# Optimizing a Trainium2 kernel written in Bass

```python
import numpy as np
import jax
import jax.numpy as jnp

def _softmax(x, axis=-1):
    return jax.nn.softmax(x, axis=axis)

def _gelu(x):
    return jax.nn.gelu(x, approximate=True)

def _silu(x):
    return jax.nn.silu(x)

def _sigmoid(x):
    return jax.nn.sigmoid(x)

def _layernorm(x, axis=-1, eps=1e-05):
    m = jnp.mean(x, axis=axis, keepdims=True)
    v = jnp.var(x, axis=axis, keepdims=True)
    return (x - m) / jnp.sqrt(v + eps)

def _scatter_add(tgt, idx, src, axis=0):
    return tgt.at[idx].add(src)

def _segment_sum(src, seg, n):
    return jax.ops.segment_sum(src, seg, n)
kernel_name = 'mk_prb_d1_jaxref_r8_ccddc9'

def setup_inputs(seed: int=0):
    np.random.seed(seed)
    _w = jnp.asarray

    def _L0_attn_setup():
        import jax, jax.numpy as jnp
        import numpy as np
        from jax.scipy.linalg import solve_triangular
        H = 256
        NK = 16
        NV = 32
        DK = 128
        DV = 128
        KCONV = 4
        CHUNK = 64
        EPS = 1e-06
        KD = NK * DK
        VD = NV * DV
        CONV_DIM = 2 * KD + VD

        def _l2norm(x, eps=1e-06):
            return x * jax.lax.rsqrt(jnp.sum(x * x, axis=-1, keepdims=True) + eps)

        def _chunk_gated_delta_rule(q, k, v, g, beta):
            B, S, Hh, _ = q.shape
            q = _l2norm(q)
            k = _l2norm(k)
            q = q.transpose(0, 2, 1, 3).astype(jnp.float32) * DK ** (-0.5)
            k = k.transpose(0, 2, 1, 3).astype(jnp.float32)
            v = v.transpose(0, 2, 1, 3).astype(jnp.float32)
            g = g.transpose(0, 2, 1).astype(jnp.float32)
            beta = beta.transpose(0, 2, 1).astype(jnp.float32)
            N = S // CHUNK
            ch = lambda x: x.reshape(B, Hh, N, CHUNK, x.shape[-1])
            q, k, v = (ch(q), ch(k), ch(v))
            g = g.reshape(B, Hh, N, CHUNK)
            beta = beta.reshape(B, Hh, N, CHUNK)
            v_beta = v * beta[..., None]
            k_beta = k * beta[..., None]
            g = jnp.cumsum(g, axis=-1)
            dg = g[..., :, None] - g[..., None, :]
            decay = jnp.tril(jnp.exp(jnp.tril(dg)))
            M = -jnp.tril(jnp.einsum('bhnik,bhnjk->bhnij', k_beta, k) * decay, k=-1)
            eye = jnp.eye(CHUNK, dtype=jnp.float32)
            T = solve_triangular(eye - M, jnp.broadcast_to(eye, M.shape), lower=True)
            v_new = jnp.einsum('bhnij,bhnjd->bhnid', T, v_beta)
            k_cumdecay = jnp.einsum('bhnij,bhnjd->bhnid', T, k_beta * jnp.exp(g)[..., None])
            lower_incl = jnp.tril(jnp.ones((CHUNK, CHUNK), bool))

            def step(state, inp):
                q_i, k_i, v_i, kcd_i, g_i, dm_i = inp
                attn = jnp.where(lower_incl, jnp.einsum('bhik,bhjk->bhij', q_i, k_i) * dm_i, 0.0)
                v_prime = jnp.einsum('bhik,bhkv->bhiv', kcd_i, state)
                vn = v_i - v_prime
                inter = jnp.einsum('bhik,bhkv->bhiv', q_i * jnp.exp(g_i)[..., None], state)
                out = inter + jnp.einsum('bhij,bhjv->bhiv', attn, vn)
                g_last = g_i[..., -1]
                state = state * jnp.exp(g_last)[..., None, None] + jnp.einsum('bhck,bhcv->bhkv', k_i * jnp.exp(g_last[..., None] - g_i)[..., None], vn)
                return (state, out)
            xs = tuple((jnp.moveaxis(x, 2, 0) for x in (q, k, v_new, k_cumdecay, g, decay)))
            state0 = jnp.zeros((B, Hh, DK, DV), jnp.float32)
            _, outs = jax.lax.scan(step, state0, xs)
            out = jnp.moveaxis(outs, 0, 2).reshape(B, Hh, S, DV)
            return out.transpose(0, 2, 1, 3)
        key = jax.random.key(seed)
        ks = jax.random.split(key, 8)
        B, S = (2, 256)
        return {'hidden_states': jax.random.normal(ks[0], (B, S, H), jnp.float32), 'W_qkvz': jax.random.normal(ks[1], (H, 2 * KD + 2 * VD), jnp.float32) * 0.02, 'W_ba': jax.random.normal(ks[2], (H, 2 * NV), jnp.float32) * 0.02, 'conv_weight': jax.random.normal(ks[3], (CONV_DIM, KCONV), jnp.float32) * 0.1, 'A_log': jax.random.normal(ks[4], (NV,), jnp.float32) * 0.1, 'dt_bias': jax.random.normal(ks[5], (NV,), jnp.float32) * 0.1, 'norm_weight': jnp.ones((DV,), jnp.float32), 'W_out': jax.random.normal(ks[6], (VD, H), jnp.float32) * 0.02}
    _L0_attn_in = _L0_attn_setup()

    def _L0_ffn_setup():
        import jax, jax.numpy as jnp
        import numpy as np
        H = 256
        NH = 16
        NOPE = 128
        ROPE = 64
        VD = 128
        QHD = NOPE + ROPE
        E = 16
        I = 176
        TOPK = 4
        NSH = 2
        SHI = I * NSH
        EPS = 1e-06
        B, S = (2, 128)

        def rmsnorm(x, w):
            return x * jax.lax.rsqrt(jnp.mean(x * x, axis=-1, keepdims=True) + EPS) * w
        key = jax.random.key(seed)
        ks = jax.random.split(key, 12)
        sd = lambda fan_in: 1.0 / np.sqrt(fan_in)
        return {'hidden_states': jax.random.normal(ks[0], (B, S, H), jnp.float32), 'positions': jnp.broadcast_to(jnp.arange(S, dtype=jnp.int32), (B, S)), 'ln1_w': jnp.ones((H,), jnp.float32), 'ln2_w': jnp.ones((H,), jnp.float32), 'q_w': jax.random.normal(ks[1], (NH * QHD, H), jnp.float32) * sd(H), 'kv_w': jax.random.normal(ks[2], (NH * (NOPE + VD) + ROPE, H), jnp.float32) * sd(H), 'o_w': jax.random.normal(ks[3], (H, NH * VD), jnp.float32) * sd(NH * VD), 'gate_w': jax.random.normal(ks[4], (E, H), jnp.float32) * sd(H), 'w1': jax.random.normal(ks[5], (E, 2 * I, H), jnp.float32) * sd(H), 'w2': jax.random.normal(ks[6], (E, H, I), jnp.float32) * sd(I), 'sh_gu_w': jax.random.normal(ks[7], (2 * SHI, H), jnp.float32) * sd(H), 'sh_down_w': jax.random.normal(ks[8], (H, SHI), jnp.float32) * sd(SHI)}
    _L0_ffn_in = _L0_ffn_setup()
    _d = {'L0_attn_hidden_states': _L0_attn_in['hidden_states'], 'L0_attn_W_qkvz': _L0_attn_in['W_qkvz'], 'L0_attn_W_ba': _L0_attn_in['W_ba'], 'L0_attn_conv_weight': _L0_attn_in['conv_weight'], 'L0_attn_A_log': _L0_attn_in['A_log'], 'L0_attn_dt_bias': _L0_attn_in['dt_bias'], 'L0_attn_norm_weight': _L0_attn_in['norm_weight'], 'L0_attn_W_out': _L0_attn_in['W_out'], 'L0_ffn_positions': _L0_ffn_in['positions'], 'L0_ffn_ln1_w': _L0_ffn_in['ln1_w'], 'L0_ffn_ln2_w': _L0_ffn_in['ln2_w'], 'L0_ffn_q_w': _L0_ffn_in['q_w'], 'L0_ffn_kv_w': _L0_ffn_in['kv_w'], 'L0_ffn_o_w': _L0_ffn_in['o_w'], 'L0_ffn_gate_w': _L0_ffn_in['gate_w'], 'L0_ffn_w1': _L0_ffn_in['w1'], 'L0_ffn_w2': _L0_ffn_in['w2'], 'L0_ffn_sh_gu_w': _L0_ffn_in['sh_gu_w'], 'L0_ffn_sh_down_w': _L0_ffn_in['sh_down_w']}
    _x0 = _d['L0_attn_hidden_states']
    _d['L0_attn_hidden_states'] = jax.random.normal(jax.random.fold_in(jax.random.key(seed), 1), (2, 512, 256), dtype=_x0.dtype)
    del _x0
    return _d

def reference(L0_attn_hidden_states, L0_attn_W_qkvz, L0_attn_W_ba, L0_attn_conv_weight, L0_attn_A_log, L0_attn_dt_bias, L0_attn_norm_weight, L0_attn_W_out, L0_ffn_positions, L0_ffn_ln1_w, L0_ffn_ln2_w, L0_ffn_q_w, L0_ffn_kv_w, L0_ffn_o_w, L0_ffn_gate_w, L0_ffn_w1, L0_ffn_w2, L0_ffn_sh_gu_w, L0_ffn_sh_down_w):

    def _L0_attn_ref(hidden_states, W_qkvz, W_ba, conv_weight, A_log, dt_bias, norm_weight, W_out):
        import jax, jax.numpy as jnp
        import numpy as np
        from jax.scipy.linalg import solve_triangular
        H = 256
        NK = 16
        NV = 32
        DK = 128
        DV = 128
        KCONV = 4
        CHUNK = 64
        EPS = 1e-06
        KD = NK * DK
        VD = NV * DV
        CONV_DIM = 2 * KD + VD

        def _l2norm(x, eps=1e-06):
            return x * jax.lax.rsqrt(jnp.sum(x * x, axis=-1, keepdims=True) + eps)

        def _chunk_gated_delta_rule(q, k, v, g, beta):
            B, S, Hh, _ = q.shape
            q = _l2norm(q)
            k = _l2norm(k)
            q = q.transpose(0, 2, 1, 3).astype(jnp.float32) * DK ** (-0.5)
            k = k.transpose(0, 2, 1, 3).astype(jnp.float32)
            v = v.transpose(0, 2, 1, 3).astype(jnp.float32)
            g = g.transpose(0, 2, 1).astype(jnp.float32)
            beta = beta.transpose(0, 2, 1).astype(jnp.float32)
            N = S // CHUNK
            ch = lambda x: x.reshape(B, Hh, N, CHUNK, x.shape[-1])
            q, k, v = (ch(q), ch(k), ch(v))
            g = g.reshape(B, Hh, N, CHUNK)
            beta = beta.reshape(B, Hh, N, CHUNK)
            v_beta = v * beta[..., None]
            k_beta = k * beta[..., None]
            g = jnp.cumsum(g, axis=-1)
            dg = g[..., :, None] - g[..., None, :]
            decay = jnp.tril(jnp.exp(jnp.tril(dg)))
            M = -jnp.tril(jnp.einsum('bhnik,bhnjk->bhnij', k_beta, k) * decay, k=-1)
            eye = jnp.eye(CHUNK, dtype=jnp.float32)
            T = solve_triangular(eye - M, jnp.broadcast_to(eye, M.shape), lower=True)
            v_new = jnp.einsum('bhnij,bhnjd->bhnid', T, v_beta)
            k_cumdecay = jnp.einsum('bhnij,bhnjd->bhnid', T, k_beta * jnp.exp(g)[..., None])
            lower_incl = jnp.tril(jnp.ones((CHUNK, CHUNK), bool))

            def step(state, inp):
                q_i, k_i, v_i, kcd_i, g_i, dm_i = inp
                attn = jnp.where(lower_incl, jnp.einsum('bhik,bhjk->bhij', q_i, k_i) * dm_i, 0.0)
                v_prime = jnp.einsum('bhik,bhkv->bhiv', kcd_i, state)
                vn = v_i - v_prime
                inter = jnp.einsum('bhik,bhkv->bhiv', q_i * jnp.exp(g_i)[..., None], state)
                out = inter + jnp.einsum('bhij,bhjv->bhiv', attn, vn)
                g_last = g_i[..., -1]
                state = state * jnp.exp(g_last)[..., None, None] + jnp.einsum('bhck,bhcv->bhkv', k_i * jnp.exp(g_last[..., None] - g_i)[..., None], vn)
                return (state, out)
            xs = tuple((jnp.moveaxis(x, 2, 0) for x in (q, k, v_new, k_cumdecay, g, decay)))
            state0 = jnp.zeros((B, Hh, DK, DV), jnp.float32)
            _, outs = jax.lax.scan(step, state0, xs)
            out = jnp.moveaxis(outs, 0, 2).reshape(B, Hh, S, DV)
            return out.transpose(0, 2, 1, 3)
        B, S, _ = hidden_states.shape
        R = NV // NK
        qkvz = (hidden_states @ W_qkvz).reshape(B, S, NK, 2 * DK + 2 * R * DV)
        ba = (hidden_states @ W_ba).reshape(B, S, NK, 2 * R)
        q = qkvz[..., :DK]
        k = qkvz[..., DK:2 * DK]
        v = qkvz[..., 2 * DK:2 * DK + R * DV].reshape(B, S, NV, DV)
        z = qkvz[..., 2 * DK + R * DV:].reshape(B, S, NV, DV)
        b = ba[..., :R].reshape(B, S, NV)
        a = ba[..., R:].reshape(B, S, NV)
        mixed = jnp.concatenate([q.reshape(B, S, -1), k.reshape(B, S, -1), v.reshape(B, S, -1)], -1)
        xp = jnp.pad(mixed, ((0, 0), (KCONV - 1, 0), (0, 0)))
        conv = sum((xp[:, j:j + S, :] * conv_weight[:, j] for j in range(KCONV)))
        mixed = jax.nn.silu(conv)
        q = mixed[..., :KD].reshape(B, S, NK, DK)
        k = mixed[..., KD:2 * KD].reshape(B, S, NK, DK)
        v = mixed[..., 2 * KD:].reshape(B, S, NV, DV)
        beta = jax.nn.sigmoid(b)
        g = -jnp.exp(A_log) * jax.nn.softplus(a + dt_bias)
        q = jnp.repeat(q, R, axis=2)
        k = jnp.repeat(k, R, axis=2)
        core = _chunk_gated_delta_rule(q, k, v, g, beta)
        x = core * jax.nn.silu(z.astype(jnp.float32))
        x = x * jax.lax.rsqrt(jnp.mean(x * x, axis=-1, keepdims=True) + EPS) * norm_weight
        return x.reshape(B, S, VD) @ W_out

    def _L0_ffn_ref(hidden_states, positions, ln1_w, ln2_w, q_w, kv_w, o_w, gate_w, w1, w2, sh_gu_w, sh_down_w):
        import jax, jax.numpy as jnp
        import numpy as np
        H = 256
        NH = 16
        NOPE = 128
        ROPE = 64
        VD = 128
        QHD = NOPE + ROPE
        E = 16
        I = 176
        TOPK = 4
        NSH = 2
        SHI = I * NSH
        EPS = 1e-06
        B, S = (2, 128)

        def rmsnorm(x, w):
            return x * jax.lax.rsqrt(jnp.mean(x * x, axis=-1, keepdims=True) + EPS) * w
        b, s, h = hidden_states.shape
        x = rmsnorm(hidden_states, ln1_w)
        q = jnp.einsum('bsh,dh->bsd', x, q_w).reshape(b, s, NH, QHD)[..., :NOPE]
        kv = jnp.einsum('bsh,dh->bsd', x, kv_w)
        k = kv[..., :NH * NOPE].reshape(b, s, NH, NOPE)
        v = kv[..., NH * NOPE:NH * (NOPE + VD)].reshape(b, s, NH, VD)
        scale = QHD ** (-0.5)
        scores = jnp.einsum('bqnd,bknd->bnqk', q, k) * scale
        causal = jnp.tril(jnp.ones((s, s), bool))
        scores = jnp.where(causal, scores, -1000000000.0)
        p = jax.nn.softmax(scores, axis=-1)
        attn = jnp.einsum('bnqk,bknd->bqnd', p, v).reshape(b, s, NH * VD)
        attn_out = jnp.einsum('bsd,hd->bsh', attn, o_w)
        hid = hidden_states + attn_out
        x2 = rmsnorm(hid, ln2_w).reshape(-1, h)
        logits = x2 @ gate_w.T
        probs = jax.nn.softmax(logits, axis=-1)
        top_w, top_i = jax.lax.top_k(probs, TOPK)
        top_w = top_w / jnp.sum(top_w, axis=-1, keepdims=True)
        wfull = jnp.sum(jax.nn.one_hot(top_i, E, dtype=x2.dtype) * top_w[..., None], axis=1)
        gu = jnp.einsum('th,eih->tei', x2, w1)
        g, u = (gu[..., :I], gu[..., I:])
        act = jax.nn.silu(g) * u
        down = jnp.einsum('tei,ehi->teh', act, w2)
        routed = jnp.einsum('te,teh->th', wfull, down)
        sgu = x2 @ sh_gu_w.T
        sg, su = (sgu[..., :SHI], sgu[..., SHI:])
        shared = jax.nn.silu(sg) * su @ sh_down_w.T
        return hid + (routed + shared).reshape(b, s, h)
    x = L0_attn_hidden_states
    xn = _layernorm(x, axis=-1)
    x = x + _L0_attn_ref(xn, L0_attn_W_qkvz, L0_attn_W_ba, L0_attn_conv_weight, L0_attn_A_log, L0_attn_dt_bias, L0_attn_norm_weight, L0_attn_W_out) + _L0_ffn_ref(xn, L0_ffn_positions, L0_ffn_ln1_w, L0_ffn_ln2_w, L0_ffn_q_w, L0_ffn_kv_w, L0_ffn_o_w, L0_ffn_gate_w, L0_ffn_w1, L0_ffn_w2, L0_ffn_sh_gu_w, L0_ffn_sh_down_w)
    return x

_drawn_inputs = setup_inputs


def setup_inputs(seed=0):
    import zlib

    import numpy as np

    out = dict(_drawn_inputs(seed))
    spreads = {'L0_attn_norm_weight': (1.0, 0.6), 'L0_ffn_ln1_w': (1.0, 0.6), 'L0_ffn_ln2_w': (1.0, 0.2)}
    factors = {'L0_attn_W_qkvz': 3.902,
     'L0_attn_W_ba': 8.0,
     'L0_attn_conv_weight': 3.872,
     'L0_attn_A_log': 8.0,
     'L0_attn_dt_bias': 8.0,
     'L0_attn_W_out': 3.905}
    for name, (base, spread) in spreads.items():
        noise = np.random.default_rng([zlib.crc32(name.encode()), seed]).standard_normal(out[name].shape)
        drawn = base * np.exp(spread * noise) if base else spread * noise
        out[name] = jnp.asarray(drawn.astype(out[name].dtype))
    for name, factor in factors.items():
        out[name] = (out[name] * factor).astype(out[name].dtype)
    return out
```

```python
from contextlib import ExitStack

import concourse.bass as bass
from concourse import mybir

P = 128
B, S, H = 2, 512, 256
TOK = B * S
NT = TOK // P
HK = H // P
NK, NV, D = 16, 32, 128
R = NV // NK
CH = 64
TAPS = 4
BL = 32
SB = 16
NC = B * R
STEPS = S // CH
NH = 16
ATT_SCALE = (128 + 64) ** -0.5
E, I, TOPK, SHI = 16, 176, 4, 352
FT = 25
FG = 5
NG = FT // FG
NEG = -1.0e30
SCORE_ORDER = (0, 2, 1, 3)

F32 = mybir.dt.float32
BF16 = mybir.dt.bfloat16
ALU = mybir.AluOpType
ACT = mybir.ActivationFunctionType
AX = mybir.AxisListType


def build(nc, d, out, debug=None):
    grow_dram = nc.dram_tensor("grow_dram", [NV + 2 * R, TOK], F32).ap()
    erow_dram = nc.dram_tensor("erow_dram", [NV + 2 * R, TOK], F32).ap()
    mt_dram = nc.dram_tensor("mt_dram", [R, NT, P, BL], F32).ap()
    tb_dram = nc.dram_tensor("tb_dram", [R, NT, 4, 2, SB * SB], F32).ap()

    with ExitStack() as ctx:
        def sb(name, shape, dt=F32):
            return ctx.enter_context(nc.sbuf_tensor(name, shape, dt))

        def sem(name):
            return ctx.enter_context(nc.semaphore(name))

        ps = ctx.enter_context(nc.psum_tensor("ps", [P, 8, 512], F32))

        ident = sb("ident", [P, P])
        total = sb("total", [P, NT, H])
        xnT = sb("xnT", [P, HK, TOK])
        gates = sb("gates", [P, NV + R, 4, NT])
        eps6 = sb("eps6", [P, 1])

        early_ctx = ExitStack()

        def early(name, shape, dt=F32):
            return early_ctx.enter_context(nc.sbuf_tensor(name, shape, dt))

        cum_mask = early("cum_mask", [P, P])
        chunk_ones = early("chunk_ones", [P, P])
        causal_neg = early("causal_neg", [P, P])
        ln1 = early("ln1", [P, HK])
        ln2 = early("ln2", [P, HK])
        xn = early("xn", [P, NT, H])
        hid = early("hid", [P, NT, H])
        xrT = early("xrT", [P, HK, TOK])
        wba = early("wba", [P, HK, 2 * NV])
        alog = early("alog", [P, NV])
        dtb = early("dtb", [P, NV])
        stats = early("stats", [P, NT, 6])
        mv = early("mv", [P, NT, 2])
        sd = early("sd", [P, NT])
        rstd = early("rstd", [P, NT])
        ssq = early("ssq", [P, NT])
        rms = early("rms", [P, NT])
        rrms = early("rrms", [P, NT])
        junk = early("junk", [P, H])
        eps5 = early("eps5", [P, 1])
        ba = early("ba", [P, NT, 2 * NV])
        ga = early("ga", [P, NT, NV])
        gb = early("gb", [P, NT, NV])
        gc = early("gc", [P, NT, NV])
        gs = early("gs", [P, NT, NV])
        g = early("g", [P, NT, NV])
        G = early("G", [P, NT, NV])
        growT = early("growT", [NV, TOK])
        erowT = early("erowT", [NV, TOK])
        wqk = early("wqk", [P, HK, 2 * P])
        wv = early("wv", [P, HK, P])
        wo = early("wo", [P, H])
        aqT = early("aqT", [P, TOK])
        akT = early("akT", [P, TOK])
        vt = early("vt", [P, NT, P])
        prob = early("prob", [P, NT, 4 * P])
        probT = early("probT", [P, NT, 4 * P])
        nmax = early("nmax", [P, NT])
        bias = early("bias", [P, NT])
        psums = early("psums", [P, NT])
        prec = early("prec", [P, NT])
        attT = early("attT", [P, TOK])
        wgate = early("wgate", [P, HK, E])
        lg = early("lg", [P, NT, E])
        lmax = early("lmax", [P, NT])
        lsum = early("lsum", [P, NT])
        lrec = early("lrec", [P, NT])
        pr = early("pr", [P, NT, E])
        before = early("before", [P, E, E])
        rank = early("rank", [P, NT, E])
        keep = early("keep", [P, NT, E])
        wfull = early("wfull", [P, NT, E + 1])
        rest = early("rest", [P, 2, NT, E + 1])
        ws = early("ws", [P, NT, 3, E + 1])
        wh = early("wh", [P, NT, 3, E + 1], BF16)
        wT = early("wT", [3 * (E + 1), TOK], BF16)
        sel = early("sel", [3 * (E + 1), FG * P], BF16)
        w13 = early("w13", [P, FG, HK, 2 * P])
        w2 = early("w2", [P, FG, H])
        sg = early("sg", [P, 2, 512])
        su = early("su", [P, 2, 512])
        act_t = early("act_t", [P, FG, TOK])
        xr = prob[:, :, 0:H]
        cmp_a = act_t[:, 0:2, :].rearrange("p a (t e f) -> p (a t) e f", e=E, f=E)
        cmp_b = act_t[:, 2:4, :].rearrange("p a (t e f) -> p (a t) e f", e=E, f=E)

        def score(b, qt):
            bank, at = ((3 * b, 0), (3 * b + 1, 0), (3 * b, P), (3 * b + 2, 0))[qt]
            return ps[:, bank, at:at + (qt + 1) * P]
        early_ctx.close()

        wA = sb("wA", [P, HK, 4 * P])
        wz = sb("wz", [P, HK, R * D])
        wout = sb("wout", [P, R, H])
        cw = sb("cw", [P, 4, TAPS])
        normw = sb("normw", [P, 1])
        cv = sb("cv", [P, 4, S])
        kT = sb("kT", [P, 2, TOK])
        qT = sb("qT", [P, TOK])
        vT = sb("vT", [P, 2, S])
        sz = sb("sz", [P, 2, B, R * D])
        junk_x = sb("junk_x", [P, NC, D])
        gh = sb("gh", [P, 2, R, 4, NT])
        Gbc = sb("Gbc", [P, R, NT, CH])
        Ebc = sb("Ebc", [P, R, TOK])
        eglast = sb("eglast", [P, 2, R, NT * 2])
        dec = sb("dec", [P, R, NT, CH])
        e_neg = sb("e_neg", [P, CH])
        eye_c = sb("eye_c", [P, CH])
        diag_k = sb("diag_k", [P, NT, CH])
        ss = sb("ss", [P, 2, NT])
        nrm = sb("nrm", [P, 2, NT])
        rk2 = sb("rk2", [P, NT])
        rq = sb("rq", [P, 2, NT])
        cb = sb("cb", [P, R, 2, NT])
        qg = sb("qg", [P, 2, R, TOK])
        MTc = sb("MTc", [P, R, NT, BL])
        MTbd = sb("MTbd", [P, R, NT, P])
        T64 = MTbd
        MOFF = sb("MOFF", [P, R, NT, P])
        blk = sb("blk", [P, SB, SB])
        Tb = sb("Tb", [P, SB, SB])
        Tprod = sb("Tprod", [P, SB, SB])
        eye16 = sb("eye16", [P, SB, SB])
        m16 = sb("m16", [P, NT * BL], mybir.dt.int32)
        half = sb("half", [P, 2])
        Tq = sb("Tq", [P, R, NT, SB])
        Tc = sb("Tc", [P, R, NT, BL])
        Xc = MTc
        TTbd = sb("TTbd", [P, R, NT, P])
        BK = sb("BK", [P, R, NT, CH + D])
        AW = sb("AW", [P, 2, R, NT, CH + D])
        vs = sb("vs", [P, 2, R, NT, D])
        St = sb("St", [P, 2, NC, D])
        Rb = sb("Rb", [P, NC, D])
        xo = sb("xo", [P, 2, NC, D])
        xT = sb("xT", [P, 2, R, TOK])
        ss2 = sb("ss2", [P, 2, R, NT])
        rms2 = sb("rms2", [P, R, NT])
        rr2 = sb("rr2", [P, R, NT])

        names = ["s_const", "s_x", "s_stat", "s_sd", "s_rstd", "s_xn", "s_ssq", "s_rms", "s_rrms", "s_xr",
                 "s_tr", "s_trE", "s_ba", "s_baE", "s_g1", "s_g2", "s_g3", "s_dch", "s_g", "s_cum", "s_G", "s_grT",
                 "s_grE", "s_st", "s_eps",
                 "s_w", "s_qk", "s_qkE", "s_v", "s_vE", "s_sc", "s_msk", "s_max", "s_bias", "s_exp", "s_rec",
                 "s_prob", "s_pT", "s_pTE", "s_pv", "s_pvE", "s_o", "s_oE", "s_ld",
                 "s_gu", "s_sg", "s_su", "s_act", "s_dn", "s_dnE",
                 "s_A", "s_tap", "s_taps", "s_conv", "s_silu", "s_gm", "s_gsub", "s_E", "s_gl", "s_pre", "s_kq", "s_ssk",
                 "s_kt", "s_kd", "s_qt", "s_sqq", "s_vt", "s_vTE", "s_nrm", "s_rr", "s_mt", "s_mtst", "s_blk", "s_solve",
                 "s_tbst", "s_tq", "s_at", "s_bd", "s_z", "s_zE", "s_qg", "s_tt", "s_xa", "s_xaE", "s_pa", "s_paE",
                 "s_tt2", "s_t64", "s_xb", "s_xbE", "s_pb", "s_pbE", "s_y", "s_yE", "s_yF", "s_p1", "s_R", "s_p2", "s_S", "s_O",
                 "s_gate", "s_sqx", "s_x2", "s_xE", "s_zero", "s_rezero", "s_wo", "s_wo1", "s_woE",
                 "s_end"]
        sm = {n: sem(n) for n in names}
        s_first, s_last = sm[names[0]].num, sm[names[-1]].num
        assert s_last - s_first == len(names) - 1
        go = {n: sem("go_" + n) for n in ("pe", "act", "dve", "pool")}

        def section_end(eng, who):
            eng.drain().then_inc(sm["s_end"], 1)
            eng.wait_ge(go[who], 1)
            eng.sem_clear(go[who])

        def section_end_sync(sp, dmas):
            for s, v in dmas:
                sp.wait_ge(sm[s], v)
            sp.wait_ge(sm["s_end"], 4)
            sp.sem_clear(range(s_first, s_last + 1))
            for who in go:
                sp.sem_inc(go[who], 1)

        def gdn_bodies(eng, body):
            with eng.Fori(0, NK // 2 - 1) as i:
                body(i, 0, False)
                body(i, 1, False)
            body(NK // 2 - 1, 0, False)
            body(NK // 2 - 1, 1, True)

        def flow_order(prepares, scans=True):
            order = ("p2 p3 z0 q0 q1 k0 k1 x0 p4 p5 z1 p6 v0 v1 p7 x1 z2 v2 v3 x2 z3 x3 y0 y1 y2 y3 y4 y5 y6 y7").split()
            return [x for x in order if (scans if x[0] in "zx" else prepares)]

        block = ctx.enter_context(nc.Block())

        @block.sync
        def _(sp):
            dma = sp.dma_start
            xv = d["x"].rearrange("(t p) h -> p t h", p=P)
            for i in range(2):
                dma(total[:, 4 * i:4 * i + 4, :], xv[:, 4 * i:4 * i + 4, :]).then_inc(sm["s_x"], 16)
            consts = [(ident, "ident"), (wba, "wba"), (alog, None), (dtb, None), (cum_mask, "cum_mask"),
                      (chunk_ones, "chunk_ones"), (ln1, "ln1"), (ln2, "ln2"), (causal_neg, "causal_neg"),
                      (wgate, "wgate"), (before, "before")]
            for t, n in consts:
                src = d[n] if n else {"alog": d["alog"], "dtb": d["dtb"]}[t.name].partition_broadcast(P)
                dma(t[:], src).then_inc(sm["s_const"], 16)
            for t, n in ((wqk, "wqk"), (wv, "wv"), (wo, "wo"), (w13, "w13"), (w2, "w2"), (sel, "sel")):
                dma(t[:], d[n][0]).then_inc(sm["s_w"], 16)
            sp.wait_ge(sm["s_grE"], 2)
            for rows, table in ((grow_dram, growT), (erow_dram, erowT)):
                dma(rows[0:NV], table[:]).then_inc(sm["s_st"], 16)
                dma(rows[NV:NV + 2 * R], table[0:2 * R]).then_inc(sm["s_st"], 16)
            section_end_sync(sp, [("s_const", 16 * len(consts)), ("s_x", 32), ("s_w", 96), ("s_st", 64)])
            sp.wait_ge(sm["s_qk"], 4)
            dma(wqk[:], d["wqk"][1]).then_inc(sm["s_ld"], 16)
            section_end_sync(sp, [("s_ld", 16)])
            with sp.Fori(0, NH) as h:
                sp.wait_ge(sm["s_v"], 2)
                dma(wv[:], d["wv"][1:][bass.ds(h, 1)]).then_inc(sm["s_ld"], 16)
                sp.wait_ge(sm["s_qk"], 4)
                dma(wqk[:], d["wqk"][2:][bass.ds(h, 1)]).then_inc(sm["s_ld"], 16)
                sp.wait_ge(sm["s_o"], 4)
                dma(wo[:], d["wo"][1:][bass.ds(h, 1)]).then_inc(sm["s_ld"], 16)
                section_end_sync(sp, [("s_ld", 48)])
            section_end_sync(sp, [])
            with sp.Fori(0, NG) as i:
                for j in range(FG):
                    sp.wait_ge(sm["s_gu"], 2 * j + 2)
                    dma(w13[:, j], d["w13"][1:][bass.ds(i, 1), :, j]).then_inc(sm["s_ld"], 16)
                sp.wait_ge(sm["s_dn"], NT)
                dma(sel[:], d["sel"][1:][bass.ds(i, 1)]).then_inc(sm["s_ld"], 16)
                dma(w2[:], d["w2"][1:][bass.ds(i, 1)]).then_inc(sm["s_ld"], 16)
                section_end_sync(sp, [("s_ld", 16 * (FG + 2))])
            first = ((wA, "wA"), (cw, "cw"), (e_neg, "e_neg"), (wz, "wz"), (normw, "normw"), (wout, "wout"),
                     (eye_c, "eye_c"), (eye16, "eye16"), (m16, "m16"), (half, "half"))
            for t, n in first:
                dma(t[:], d[n][0] if n in ("wA", "cw", "wz", "wout") else d[n]).then_inc(sm["s_w"], 16)

            def decays_of(h):
                rows = grow_dram.rearrange("(k r) (t c i) -> k c r t i", r=R, c=2, i=CH)
                for c in range(2):
                    src = rows[h, c] if isinstance(h, int) else rows[h, c].squeeze(0)
                    dma(Gbc[c * CH:(c + 1) * CH], src.partition_broadcast(CH)).then_inc(sm["s_gl"], 16)

            def exponentials_of(h):
                rows = erow_dram.rearrange("(k r) n -> k r n", r=R)
                src = rows[h] if isinstance(h, int) else rows[h].squeeze(0)
                dma(Ebc[:], src.partition_broadcast(P)).then_inc(sm["s_gl"], 16)

            decays_of(0)
            exponentials_of(0)

            def blocks_out_and_back():
                for r in range(R):
                    sp.wait_ge(sm["s_mt"], r + 1)
                    dma(mt_dram[r].rearrange("t p i -> p t i"), MTc[:, r]).then_inc(sm["s_mtst"], 16)
                sp.wait_ge(sm["s_mtst"], 16 * R)
                for r in range(R):
                    for s in range(2):
                        src = mt_dram[r].rearrange("t (q s j) (w i) -> s w (t q) j i", s=2, j=SB, w=2)[s, s]
                        dma(blk[r * 64 + s * 32:r * 64 + (s + 1) * 32], src).then_inc(sm["s_blk"], 16)
                sp.wait_ge(sm["s_solve"], 1)
                for r in range(R):
                    for s in range(2):
                        dma(tb_dram[r].rearrange("t q s x -> s (t q) x")[s],
                            Tb[r * 64 + s * 32:r * 64 + (s + 1) * 32].rearrange("p i j -> p (i j)")).then_inc(sm["s_tbst"], 16)
                sp.wait_ge(sm["s_tbst"], 16 * 2 * R)
                for r in range(R):
                    dma(Tq[:, r], tb_dram[r].rearrange("t q s (i j) -> (q s i) t j", j=SB)).then_inc(sm["s_tq"], 16)

            def ahead(slot, new_z):
                sp.wait_ge(sm["s_A"], 8)
                dma(wA[:], d["wA"][slot(2)]).then_inc(sm["s_ld"], 16)
                sp.wait_ge(sm["s_conv"], 8)
                dma(cw[:], d["cw"][slot(2)]).then_inc(sm["s_ld"], 16)
                if new_z:
                    sp.wait_ge(sm["s_z"], 4)
                    dma(wz[:], d["wz"][slot(1)]).then_inc(sm["s_ld"], 16)
                    sp.wait_ge(sm["s_wo"], NT)
                    dma(wout[:], d["wout"][slot(1)]).then_inc(sm["s_ld"], 16)

            sp.wait_ge(sm["s_gm"], 1)
            decays_of(1)
            sp.wait_ge(sm["s_qg"], R)
            sp.wait_ge(sm["s_pre"], 1)
            exponentials_of(1)
            blocks_out_and_back()
            ahead(lambda n: n - 1, False)
            section_end_sync(sp, [("s_w", 16 * len(first)), ("s_gl", 16 * 6), ("s_ld", 32), ("s_blk", 64), ("s_tq", 32)])

            def gdn_body(i, par, last):
                if not last:
                    def slot(n):
                        return 2 * i + par + n if isinstance(i, int) else bass.ds(i * 2 + (par + n), 1)

                    decays_of(slot(2))
                    sp.wait_ge(sm["s_qg"], R)
                    exponentials_of(slot(2))
                    blocks_out_and_back()
                    ahead(slot, True)
                    section_end_sync(sp, [("s_gl", 48), ("s_ld", 64), ("s_blk", 64), ("s_tq", 32)])
                else:
                    sp.wait_ge(sm["s_wo"], NT)
                    dma(wout[:], d["wout"][NK]).then_inc(sm["s_ld"], 16)
                    section_end_sync(sp, [("s_ld", 16)])

            gdn_bodies(sp, gdn_body)
            section_end_sync(sp, [])
            dma(out.rearrange("(t p) h -> p t h", p=P), total[:]).then_inc(sm["s_st"], 16)
            sp.wait_ge(sm["s_st"], 16)

        @block.tensor
        def _(pe):
            mm = pe.matmul

            pe.wait_ge(sm["s_const"], 16 * 11)
            for src, sname, base in ((xn, "s_xn", 0), (xr, "s_xr", 4)):
                for k in range(HK):
                    for n in range(2):
                        pe.wait_ge(sm[sname], 4 * n + 4)
                        for i in range(4):
                            last = pe.transpose(ps[:, base + 2 * k + n, i * P:(i + 1) * P],
                                                src[:, 4 * n + i, k * P:(k + 1) * P], ident[:])
                        last.then_inc(sm["s_tr"], 1)
            pe.wait_ge(sm["s_trE"], 8)
            for t in range(NT):
                for k in range(HK):
                    last = mm(ps[:, 0, t * 2 * NV:(t + 1) * 2 * NV], xnT[:, k, t * P:(t + 1) * P], wba[:, k, :],
                              start=(k == 0), stop=(k == HK - 1))
            last.then_inc(sm["s_ba"], 1)
            pe.wait_ge(sm["s_g"], 1)
            g_all = g[:].rearrange("p t v -> p (t v)")
            mm(ps[:, 1, 0:NT * NV], cum_mask[:], g_all, start=True, stop=True).then_inc(sm["s_cum"], 1)
            mm(ps[:, 2, 0:NT * NV], chunk_ones[:], g_all, start=True, stop=True).then_inc(sm["s_cum"], 1)
            pe.wait_ge(sm["s_G"], 1)
            for t in range(NT):
                last = pe.transpose(ps[0:NV, 3 + t // 4, (t % 4) * P:(t % 4 + 1) * P], G[:, t, :], ident[:])
                if t % 4 == 3:
                    last.then_inc(sm["s_grT"], 1)
            section_end(pe, "pe")

            def project_qk():
                for j in range(4):
                    w, n = j // 2, j % 2
                    if j >= 2:
                        pe.wait_ge(sm["s_qkE"], j - 1)
                    for k in range(HK):
                        last = mm(ps[:, 6 + j % 2, :], wqk[:, k, w * P:(w + 1) * P], xrT[:, k, n * 512:(n + 1) * 512],
                                  start=(k == 0), stop=(k == HK - 1))
                    last.then_inc(sm["s_qk"], 1)

            project_qk()
            section_end(pe, "pe")
            with pe.Fori(0, NH) as h:
                for b in range(B):
                    for qt in SCORE_ORDER:
                        q = (4 * b + qt) * P
                        last = mm(score(b, qt), aqT[:, q:q + P], akT[:, b * S:b * S + (qt + 1) * P],
                                  start=True, stop=True)
                        last.then_inc(sm["s_sc"], 1)
                for n in range(2):
                    for t in range(4 * n, 4 * n + 4):
                        for k in range(HK):
                            last = mm(ps[:, 6 + n, (t % 4) * P:(t % 4 + 1) * P], xrT[:, k, t * P:(t + 1) * P],
                                      wv[:, k, :], start=(k == 0), stop=(k == HK - 1))
                    last.then_inc(sm["s_v"], 1)
                pe.wait_ge(sm["s_vE"], 2)
                project_qk()
                for b in range(B):
                    pe.wait_ge(sm["s_exp"], 4 * b + 4)
                    pe.wait_ge(sm["s_prob"], 4 * b + 4)
                    for kt in range(4):
                        if kt == 3:
                            pe.wait_ge(sm["s_pTE"], 4 * b + 1)
                        for qt in range(kt, 4):
                            last = pe.transpose(ps[:, 3 * b + kt % 3, qt * P:(qt + 1) * P],
                                                prob[:, 4 * b + qt, kt * P:(kt + 1) * P], ident[:])
                        last.then_inc(sm["s_pT"], 1)
                pe.wait_ge(sm["s_qkE"], 4)
                for b in range(B):
                    for kt in range(4):
                        pe.wait_ge(sm["s_pTE"], 4 * b + kt + 1)
                        last = mm(ps[:, 6 + b, kt * P:S], vt[:, 4 * b + kt, :], probT[:, 4 * b + kt, kt * P:S],
                                  start=(kt == 0), stop=(kt == 3), skip_group_check=True)
                    last.then_inc(sm["s_pv"], 1)
                for t in range(NT):
                    if t % 4 == 0:
                        pe.wait_ge(sm["s_pvE"], t // 4 + 1)
                    last = mm(ps[:, t // 2, (t % 2) * H:(t % 2 + 1) * H], attT[:, t * P:(t + 1) * P], wo[:],
                              start=True, stop=True)
                    if t % 2:
                        last.then_inc(sm["s_o"], 1)
                section_end(pe, "pe")

            for k in range(HK):
                for n in range(2):
                    pe.wait_ge(sm["s_xr"], 4 * n + 4)
                    for i in range(4):
                        last = pe.transpose(ps[:, 2 * k + n, i * P:(i + 1) * P],
                                            xr[:, 4 * n + i, k * P:(k + 1) * P], ident[:])
                    last.then_inc(sm["s_tr"], 1)
            pe.wait_ge(sm["s_trE"], 4)
            for t in range(NT):
                for k in range(HK):
                    last = mm(ps[:, 4, t * E:(t + 1) * E], xrT[:, k, t * P:(t + 1) * P], wgate[:, k, :],
                              start=(k == 0), stop=(k == HK - 1))
            last.then_inc(sm["s_ba"], 1)
            pe.wait_ge(sm["s_g"], 1)
            for t in range(NT):
                last = pe.transpose(ps[0:3 * (E + 1), 5 + t // 4, (t % 4) * P:(t % 4 + 1) * P],
                                    ws[:, t].rearrange("p a e -> p (a e)"), ident[:])
                if t % 4 == 3:
                    last.then_inc(sm["s_grT"], 1)
            section_end(pe, "pe")

            with pe.Fori(0, NG) as i:
                for j in range(FG):
                    for n in range(2):
                        u = 2 * j + n
                        cols = slice(n * 512, (n + 1) * 512)
                        if j:
                            pe.wait_ge(sm["s_act"], u - 1)
                        for part in range(2):
                            for k in range(HK):
                                last = mm(ps[:, 3 * n + part, :], w13[:, j, k, part * P:(part + 1) * P], xrT[:, k, cols],
                                          start=(k == 0), stop=(k == HK - 1))
                        mm(ps[:, 3 * n + 2, :], sel[:, j * P:(j + 1) * P], wT[:, cols],
                           start=True, stop=True).then_inc(sm["s_gu"], 1)
                for t in range(NT):
                    if t == 0:
                        pe.wait_ge(sm["s_act"], 2 * FG)
                    if t >= 2:
                        pe.wait_ge(sm["s_dnE"], t - 1)
                    for j in range(FG):
                        last = mm(ps[:, 6 + t % 2, 0:H], act_t[:, j, t * P:(t + 1) * P], w2[:, j, :],
                                  start=(j == 0), stop=(j == FG - 1))
                    last.then_inc(sm["s_dn"], 1)
                section_end(pe, "pe")

            def flow_bank(flow, evacuated):
                if len(flow) >= 2:
                    s, v = flow[-2]
                    pe.wait_ge(sm[s], v)
                flow.append(evacuated)
                return 6 + (len(flow) - 1) % 2

            def transposes(bank, sources, s):
                for i, src in enumerate(sources):
                    last = pe.transpose(ps[:, bank, i * P:(i + 1) * P], src, ident[:])
                last.then_inc(sm[s], 1)

            def project(flow, u):
                i, b = (1, 0, 2, 3)[u // 2], u % 2
                bank = 4 + u if u < 2 else flow_bank(flow, ("s_conv", u + 1))
                for k in range(HK):
                    last = mm(ps[:, bank, :], wA[:, k, i * P:(i + 1) * P], xnT[:, k, b * S:(b + 1) * S],
                              start=(k == 0), stop=(k == HK - 1))
                last.then_inc(sm["s_A"], 1)

            def key_products(nx):
                pe.wait_ge(sm["s_silu"], 4)
                for t in range(NT):
                    for c in range(2):
                        at = t * P + c * CH
                        for i, x in enumerate((kT[:, nx], qT)):
                            last = mm(ps[c * CH:(c + 1) * CH, 4 + t // 4, (t % 4) * P + i * CH:(t % 4) * P + (i + 1) * CH],
                                      kT[:, nx, at:at + CH], x[:, at:at + CH], start=True, stop=True)
                last.then_inc(sm["s_kq"], 1)

            def turn_keys(flow, nx, n):
                bank = flow_bank(flow, ("s_kd", n + 1))
                transposes(bank, [kT[:, nx, t * P:(t + 1) * P] for t in range(4 * n, 4 * n + 4)], "s_kt")

            def turn_queries(flow, n):
                bank = flow_bank(flow, ("s_sqq", n + 1))
                transposes(bank, [qT[:, t * P:(t + 1) * P] for t in range(4 * n, 4 * n + 4)], "s_qt")

            def turn_values(flow, u):
                pe.wait_ge(sm["s_silu"], 5 + u)
                bank = flow_bank(flow, ("s_vTE", u + 1))
                transposes(bank, [vT[:, u % 2, t * P:(t + 1) * P] for t in range(4)], "s_vt")

            def gate_product(flow, m):
                bank = flow_bank(flow, ("s_zE", m + 1))
                for b in range(B):
                    at = b * S + m * P
                    for k in range(HK):
                        last = mm(ps[:, bank, b * R * D:(b + 1) * R * D], xnT[:, k, at:at + P], wz[:, k, :],
                                  start=(k == 0), stop=(k == HK - 1))
                last.then_inc(sm["s_z"], 1)

            def turn_outputs(flow, m):
                pe.wait_ge(sm["s_gate"], 2 * m + 2)
                bank = flow_bank(flow, ("s_xE", m + 1))
                transposes(bank, [xo[:, m % 2, b * R + r, :] for r in range(R) for b in range(B)], "s_x")

            def output_product(par, t):
                if t >= 2:
                    pe.wait_ge(sm["s_woE"], t - 1)
                for r in range(R):
                    last = mm(ps[:, 4 + t % 2, r * H:(r + 1) * H], xT[:, 1 - par, r, t * P:(t + 1) * P],
                              wout[:, r, :], start=True, stop=True)
                last.then_inc(sm["s_wo"], 1)

            def level(lhs, rhs, at, s, ready):
                for r in range(R):
                    for sname, v in ready:
                        pe.wait_ge(sm[sname], v(r))
                    for t in range(NT):
                        last = mm(ps[:, 4 + r, at + t * BL:at + (t + 1) * BL], lhs[:, r, t, :], rhs[:, r, t, :],
                                  start=True, stop=True)
                    last.then_inc(sm[s], 1)

            def blocks_of_32():
                level(MTbd, Tc, 0, "s_xa", [("s_bd", lambda r: 4 * R), ("s_tt", lambda r: r + 1)])
                level(TTbd, Xc, 256, "s_pa", [("s_xaE", lambda r: r + 1)])

            def chunks_from_32():
                level(MOFF, Tc, 0, "s_xb", [("s_paE", lambda r: r + 1)])
                level(TTbd, Xc, 256, "s_pb", [("s_xbE", lambda r: r + 1), ("s_tt2", lambda r: r + 1)])

            def solve_products(flow):
                for u in range(R * NT // 2):
                    r, m = u // 4, u % 4
                    pe.wait_ge(sm["s_pbE"], r + 1)
                    bank = flow_bank(flow, (("s_yE", "s_yF")[u % 2], u // 2 + 1))
                    for i in range(2):
                        last = mm(ps[:, bank, i * (CH + D):(i + 1) * (CH + D)], T64[:, r, 2 * m + i, :],
                                  BK[:, r, 2 * m + i, :], start=True, stop=True)
                    last.then_inc(sm["s_y"], 1)

            flow = []
            pe.wait_ge(sm["s_w"], 16 * 10)
            for u in range(4):
                project(flow, u)
            key_products(0)
            for n in range(2):
                turn_queries(flow, n)
            for n in range(2):
                turn_keys(flow, 0, n)
            for u in (4, 5, 6):
                project(flow, u)
            for u in (0, 1):
                turn_values(flow, u)
            project(flow, 7)
            for u in (2, 3):
                turn_values(flow, u)
            pe.wait_ge(sm["s_at"], R)
            blocks_of_32()
            chunks_from_32()
            solve_products(flow)
            section_end(pe, "pe")

            def gdn_body(i, par, last_body):
                nx = 1 - par
                flow = []

                def pre(f, *a):
                    if not last_body:
                        f(*a)

                def key_state(n, b):
                    pe.wait_ge(sm["s_S"], 2 * (n - 1) + b + 1)
                    rows = slice((n % 2) * CH, (n % 2 + 1) * CH)
                    at = b * S + n * CH
                    for r in range(R):
                        last = mm(ps[rows, b, r * D:(r + 1) * D], kT[:, par, at:at + CH], St[:, n % 2, b * R + r, :],
                                  start=True, stop=True)
                    last.then_inc(sm["s_p1"], 1)

                def residual(n, b, r):
                    rows = slice((n % 2) * CH, (n % 2 + 1) * CH)
                    return Rb[rows, b * R + r, :] if n else vs[rows, par, r, 4 * b, :]

                def new_state(n, b):
                    if n:
                        pe.wait_ge(sm["s_R"], 2 * (n - 1) + b + 1)
                    rows = slice((n % 2) * CH, (n % 2 + 1) * CH)
                    for r in range(R):
                        last = mm(ps[:, b, (R + r) * D:(R + r + 1) * D], AW[rows, par, r, 4 * b + n // 2, CH:],
                                  residual(n, b, r), start=True, stop=True)
                    last.then_inc(sm["s_p2"], 1)

                def chunk_output(n, b):
                    m, rows, at = n // 2, slice((n % 2) * CH, (n % 2 + 1) * CH), b * S + n * CH
                    if n == STEPS - 1:
                        pe.wait_ge(sm["s_R"], 2 * (n - 1) + b + 1)
                    if n % 2 == 0 and m:
                        pe.wait_ge(sm["s_gate"], 2 * (m - 1) + b + 1)
                    for r in range(R):
                        dst = ps[rows, 2 + b, r * D:(r + 1) * D]
                        if n:
                            mm(dst, qg[:, par, r, at:at + CH], St[:, n % 2, b * R + r, :], start=True, stop=False)
                        last = mm(dst, AW[rows, par, r, 4 * b + m, 0:CH], residual(n, b, r), start=(n == 0), stop=True)
                    last.then_inc(sm["s_O"], 1)

                def beside_residuals(n):
                    if n == 0:
                        for u in (0, 1):
                            pre(project, flow, u)
                    if n == 1:
                        gate_product(flow, 0)
                    if n == 2:
                        pre(key_products, nx)
                    if n == 3:
                        turn_outputs(flow, 0)
                    if n == 4:
                        gate_product(flow, 1)
                    if n == 5:
                        pre(turn_values, flow, 1)
                    if n == 6:
                        turn_outputs(flow, 1)
                        gate_product(flow, 2)
                    if n == 7:
                        turn_outputs(flow, 2)
                        gate_product(flow, 3)

                def beside_states(n):
                    if n == 0:
                        for u in (2, 3):
                            pre(project, flow, u)
                    if n == 2:
                        for k in range(2):
                            pre(turn_queries, flow, k)
                        for k in range(2):
                            pre(turn_keys, flow, nx, k)
                    if n == 3:
                        for u in (4, 5):
                            pre(project, flow, u)
                    if n == 4:
                        pre(project, flow, 6)
                        pre(turn_values, flow, 0)
                    if n == 5:
                        pre(project, flow, 7)

                for n in range(STEPS):
                    if n:
                        for b in range(B):
                            key_state(n, b)
                    beside_residuals(n)
                    if n < STEPS - 1:
                        for b in range(B):
                            new_state(n, b)
                    beside_states(n)
                    for b in range(B):
                        chunk_output(n, b)
                    if n == 6:
                        for t in range(4):
                            output_product(par, t)
                        for u in (2, 3):
                            pre(turn_values, flow, u)
                        for t in range(4, 8):
                            output_product(par, t)
                turn_outputs(flow, 3)
                pe.wait_ge(sm["s_woE"], NT)
                pre(blocks_of_32)
                pre(chunks_from_32)
                pre(solve_products, flow)
                section_end(pe, "pe")

            gdn_bodies(pe, gdn_body)
            for t in range(NT):
                output_product(0, t)
            section_end(pe, "pe")

        @block.scalar
        def _(act):
            fn = act.activation

            act.wait_ge(sm["s_eps"], 2)
            act.wait_ge(sm["s_stat"], 1)
            fn(sd[:], mv[:, :, 1], ACT.Sqrt, bias=eps5[:]).then_inc(sm["s_sd"], 1)
            for t in range(NT):
                act.wait_ge(sm["s_xn"], t + 1)
                if t:
                    act.wait_ge(sm["s_ssq"], t)
                fn(junk[:], xn[:, t, :], ACT.Square, accum_out=ssq[:, t:t + 1]).then_inc(sm["s_ssq"], 1)
            act.wait_ge(sm["s_ssq"], NT)
            fn(rms[:], ssq[:], ACT.Sqrt, bias=eps6[:], scale=1.0 / H).then_inc(sm["s_rms"], 1)
            for i in range(4):
                act.wait_ge(sm["s_tr"], i + 1)
                fn(xnT[:, i // 2, (i % 2) * 512:(i % 2 + 1) * 512], ps[:, i, :], ACT.Copy).then_inc(sm["s_trE"], 1)
            act.wait_ge(sm["s_g1"], 2)
            fn(gb[:], gb[:], ACT.Exp, scale=-1.0).then_inc(sm["s_g2"], 1)
            fn(gs[:], ba[:, :, 0:NV], ACT.Exp, scale=-1.0).then_inc(sm["s_g2"], 1)
            fn(alog[:], alog[:], ACT.Exp).then_inc(sm["s_g2"], 1)
            act.wait_ge(sm["s_g2"], 3)
            fn(gb[:], gb[:], ACT.Ln, bias=1.0).then_inc(sm["s_g3"], 1)
            act.wait_ge(sm["s_G"], 2)
            fn(ga[:], G[:], ACT.Exp).then_inc(sm["s_g2"], 1)
            fn(gc[:], gc[:], ACT.Exp).then_inc(sm["s_g2"], 1)
            act.wait_ge(sm["s_grT"], 2)
            fn(growT[:], ps[0:NV, 3:5, :].rearrange("p a n -> p (a n)"), ACT.Copy).then_inc(sm["s_grE"], 1)
            fn(erowT[:], ps[0:NV, 3:5, :].rearrange("p a n -> p (a n)"), ACT.Exp).then_inc(sm["s_grE"], 1)
            section_end(act, "act")

            def take_qk():
                for j in range(4):
                    act.wait_ge(sm["s_qk"], j + 1)
                    dst = (aqT, akT)[j // 2]
                    fn(dst[:, (j % 2) * 512:(j % 2 + 1) * 512], ps[:, 6 + j % 2, :], ACT.Copy).then_inc(sm["s_qkE"], 1)

            take_qk()
            section_end(act, "act")
            with act.Fori(0, NH) as h:
                for b in range(B):
                    act.wait_ge(sm["s_bias"], b + 1)
                    for qt in range(4):
                        u = 4 * b + qt
                        fn(prob[:, u, 0:(qt + 1) * P], score(b, qt), ACT.Exp, bias=bias[:, u:u + 1],
                           scale=ATT_SCALE, accum_out=psums[:, u:u + 1]).then_inc(sm["s_exp"], 1)
                    if b == 0:
                        take_qk()
                for b in range(B):
                    for kt in range(4):
                        act.wait_ge(sm["s_pT"], 4 * b + kt + 1)
                        fn(probT[:, 4 * b + kt, kt * P:S], ps[:, 3 * b + kt % 3, kt * P:S], ACT.Copy).then_inc(sm["s_pTE"], 1)
                for b in range(B):
                    act.wait_ge(sm["s_pv"], b + 1)
                    fn(attT[:, b * S:(b + 1) * S], ps[:, 6 + b, :], ACT.Copy).then_inc(sm["s_pvE"], 1)
                section_end(act, "act")

            for t in range(NT):
                if t:
                    act.wait_ge(sm["s_ssq"], t)
                fn(junk[:], hid[:, t, :], ACT.Square, accum_out=ssq[:, t:t + 1]).then_inc(sm["s_ssq"], 1)
            act.wait_ge(sm["s_ssq"], NT)
            fn(rms[:], ssq[:], ACT.Sqrt, bias=eps6[:], scale=1.0 / H).then_inc(sm["s_rms"], 1)
            for i in range(4):
                act.wait_ge(sm["s_tr"], i + 1)
                k, n = i // 2, i % 2
                fn(xrT[:, k, n * 512:(n + 1) * 512], ps[:, i, :], ACT.Copy, scale=ln2[:, k:k + 1]).then_inc(sm["s_trE"], 1)
            act.wait_ge(sm["s_g1"], 1)
            fn(lg[:], lg[:], ACT.Exp).then_inc(sm["s_g2"], 1)
            section_end(act, "act")

            with act.Fori(0, NG) as i:
                for u in range(2 * FG):
                    act.wait_ge(sm["s_gu"], u + 1)
                    if u >= 2:
                        act.wait_ge(sm["s_su"], u - 1)
                    fn(sg[:, u % 2, :], ps[:, 3 * (u % 2), :], ACT.Silu).then_inc(sm["s_sg"], 1)
                section_end(act, "act")

            def tap(u, bank):
                i = (1, 0, 2, 3)[u // 2]
                act.wait_ge(sm["s_A"], u + 1)
                if u >= 4:
                    act.wait_ge(sm["s_silu"], u - 3)
                fn(cv[:, u % 4, :], ps[:, bank, :], ACT.Copy, scale=cw[:, i, TAPS - 1:TAPS]).then_inc(sm["s_tap"], 1)

            def silu(u, nx):
                b = u % 2
                dst = (kT[:, nx, b * S:(b + 1) * S], qT[:, b * S:(b + 1) * S], vT[:, b, :], vT[:, b, :])[u // 2]
                act.wait_ge(sm["s_conv"], u + 1)
                if u >= 6:
                    act.wait_ge(sm["s_vt"], u - 5)
                fn(dst, cv[:, u % 4, :], ACT.Silu).then_inc(sm["s_silu"], 1)

            def decays():
                act.wait_ge(sm["s_gsub"], 1)
                fn(dec[:], dec[:], ACT.Exp).then_inc(sm["s_E"], 1)

            def query_squares(n, bank):
                act.wait_ge(sm["s_qt"], n + 1)
                for t in range(4 * n, 4 * n + 4):
                    q = ps[:, bank, (t % 4) * P:(t % 4 + 1) * P]
                    last = fn(q, q, ACT.Square, accum_out=ss[:, 1, t:t + 1])
                last.then_inc(sm["s_sqq"], 1)

            def norms():
                act.wait_ge(sm["s_ssk"], 1)
                act.wait_ge(sm["s_sqq"], 2)
                fn(nrm[:], ss[:], ACT.Sqrt, bias=eps6[:]).then_inc(sm["s_nrm"], 1)

            def output_rms(par):
                fn(rms2[:], ss2[:, 1 - par], ACT.Sqrt, bias=eps6[:], scale=1.0 / D).then_inc(sm["s_nrm"], 1)

            def gate_silu(m, bank):
                act.wait_ge(sm["s_z"], m + 1)
                if m >= 2:
                    act.wait_ge(sm["s_gate"], 2 * (m - 1))
                fn(sz[:, m % 2].rearrange("p b d -> p (b d)"), ps[:, bank, :], ACT.Silu).then_inc(sm["s_zE"], 1)

            def output_squares(par, m):
                for b in range(B):
                    act.wait_ge(sm["s_gate"], 2 * m + b + 1)
                    for r in range(R):
                        if m:
                            act.wait_ge(sm["s_sqx"], 4 * (m - 1) + 2 * b + r + 1)
                        fn(junk_x[:, b * R + r, :], xo[:, m % 2, b * R + r, :], ACT.Square,
                           accum_out=ss2[:, par, r, 4 * b + m:4 * b + m + 1]).then_inc(sm["s_sqx"], 1)

            def outputs_turned(par, m, bank):
                act.wait_ge(sm["s_x"], m + 1)
                dst = xT[:, par].rearrange("p r (b n) -> p (r b) n", b=B)[:, :, m * P:(m + 1) * P]
                fn(dst, ps[:, bank, :].rearrange("p (a n) -> p a n", a=NC), ACT.Copy, scale=normw[:]).then_inc(sm["s_xE"], 1)

            def take_x(r, src, dst):
                act.wait_ge(sm[src], r + 1)
                fn(Xc[:, r], ps[:, 4 + r, 0:256].rearrange("p (t c) -> p t c", c=BL), ACT.Copy).then_inc(sm[dst], 1)

            def last_blocks(r):
                act.wait_ge(sm["s_pb"], r + 1)
                act.wait_ge(sm["s_t64"], r + 1)
                for q in (1, 3):
                    last = fn(T64[q * BL:(q + 1) * BL, r, :, (q - 1) * BL:q * BL],
                              ps[q * BL:(q + 1) * BL, 4 + r, 256:512].rearrange("p (t c) -> p t c", c=BL), ACT.Copy)
                last.then_inc(sm["s_pbE"], 1)

            def take_products(u, nx):
                r, m = u // 4, u % 4
                act.wait_ge(sm["s_y"], u + 1)
                fn(AW[:, nx, r, 2 * m:2 * m + 2, :],
                   ps[:, 6 + u % 2, 0:2 * (CH + D)].rearrange("p (t d) -> p t d", t=2), ACT.Copy).then_inc(sm["s_yE"], 1)

            def solved(nx):
                for r in range(R):
                    take_x(r, "s_xa", "s_xaE")
                for r in range(R):
                    take_x(r, "s_xb", "s_xbE")
                for r in range(R):
                    last_blocks(r)
                for u in range(0, 8, 2):
                    take_products(u, nx)

            def bank_in(order, x):
                return {"p0": 4, "p1": 5}[x] if x in ("p0", "p1") else 6 + order.index(x) % 2

            order = flow_order(True, False)
            act.wait_ge(sm["s_w"], 16 * 10)
            decays()
            for u in range(4):
                tap(u, bank_in(order, "p%d" % u))
                silu(u, 0)
            for n in range(2):
                query_squares(n, bank_in(order, "q%d" % n))
            norms()
            for u in (4, 5):
                tap(u, bank_in(order, "p%d" % u))
                silu(u, 0)
            for u in (6, 7):
                tap(u, bank_in(order, "p%d" % u))
                silu(u, 0)
            act.wait_ge(sm["s_gsub"], 2)
            fn(dec[:], dec[:], ACT.Exp)
            solved(0)
            section_end(act, "act")

            def gdn_body(i, par, last_body):
                nx = 1 - par
                order = flow_order(not last_body)

                def bank(x):
                    return bank_in(order, x)

                def taps(*units):
                    for u in units:
                        if not last_body:
                            tap(u, bank("p%d" % u))

                def silus(*units):
                    for u in units:
                        if not last_body:
                            silu(u, nx)

                taps(0, 1, 2, 3)
                silus(0, 1, 2)
                gate_silu(0, bank("z0"))
                silus(3)
                if not last_body:
                    query_squares(0, bank("q0"))
                    query_squares(1, bank("q1"))
                    norms()
                output_rms(par)
                output_squares(par, 0)
                outputs_turned(par, 0, bank("x0"))
                taps(4, 5)
                silus(4)
                gate_silu(1, bank("z1"))
                silus(5)
                taps(6)
                silus(6)
                taps(7)
                output_squares(par, 1)
                outputs_turned(par, 1, bank("x1"))
                silus(7)
                gate_silu(2, bank("z2"))
                output_squares(par, 2)
                outputs_turned(par, 2, bank("x2"))
                gate_silu(3, bank("z3"))
                if not last_body:
                    decays()
                output_squares(par, 3)
                outputs_turned(par, 3, bank("x3"))
                if not last_body:
                    solved(nx)
                section_end(act, "act")

            gdn_bodies(act, gdn_body)
            output_rms(0)
            section_end(act, "act")

        @block.vector
        def _(dve):
            tt, ts, stt = dve.tensor_tensor, dve.tensor_scalar, dve.scalar_tensor_tensor
            steps = [0]

            def step(ins):
                steps[0] += 1
                ins.then_inc(sm["s_dch"], 1)
                dve.wait_ge(sm["s_dch"], steps[0])

            def end():
                steps[0] = 0
                section_end(dve, "dve")

            for t in range(NT):
                dve.wait_ge(sm["s_x"], 32)
                step(dve.bn_stats(stats[:, t, :], total[:, t, :]))
            for t in range(NT):
                last = dve.bn_aggr(mv[:, t, :], stats[:, t, :])
            last.then_inc(sm["s_stat"], 1)
            dve.wait_ge(sm["s_sd"], 1)
            step(dve.reciprocal(rstd[:], sd[:]))
            for t in range(NT):
                ts(xn[:, t, :], total[:, t, :], mv[:, t, 0:1], rstd[:, t:t + 1], ALU.subtract,
                   ALU.mult).then_inc(sm["s_xn"], 1)
            dve.wait_ge(sm["s_rms"], 1)
            step(dve.reciprocal(rrms[:], rms[:]))
            for t in range(NT):
                ts(xr[:, t, :], xn[:, t, :], rrms[:, t:t + 1], None, ALU.mult).then_inc(sm["s_xr"], 1)
            dve.wait_ge(sm["s_const"], 16 * 11)
            for i in range(4):
                dve.wait_ge(sm["s_tr"], 5 + i)
                k, n = i // 2, i % 2
                ts(xrT[:, k, n * 512:(n + 1) * 512], ps[:, 4 + i, :], ln1[:, k:k + 1], None,
                   ALU.mult).then_inc(sm["s_trE"], 1)
            dve.wait_ge(sm["s_ba"], 1)
            step(dve.tensor_copy(ba[:], ps[:, 0, :].rearrange("p (t v) -> p t v", t=NT)))
            step(tt(ga[:], ba[:, :, NV:2 * NV], dtb[:].unsqueeze(1).broadcast_to([P, NT, NV]), ALU.add))
            step(ts(gc[:], ga[:], -1.0, None, ALU.mult))
            tt(gb[:], ga[:], gc[:], ALU.max).then_inc(sm["s_g1"], 1)
            ts(ga[:], ga[:], 0.0, None, ALU.max).then_inc(sm["s_g1"], 1)
            dve.wait_ge(sm["s_g2"], 3)
            step(ts(gs[:], gs[:], 1.0, None, ALU.add))
            step(dve.reciprocal(gs[:], gs[:]))
            dve.wait_ge(sm["s_g3"], 1)
            step(tt(ga[:], ga[:], gb[:], ALU.add))
            stt(g[:], ga[:], -1.0, alog[:].unsqueeze(1).broadcast_to([P, NT, NV]), ALU.mult,
                ALU.mult).then_inc(sm["s_g"], 1)
            dve.wait_ge(sm["s_cum"], 2)
            cum, last_sum = (ps[:, i, 0:NT * NV].rearrange("p (t v) -> p t v", t=NT) for i in (1, 2))
            dve.tensor_copy(G[:], cum).then_inc(sm["s_G"], 1)
            dve.wait_ge(sm["s_G"], 1)
            tt(gc[:], last_sum, G[:], ALU.subtract).then_inc(sm["s_G"], 1)
            dve.wait_ge(sm["s_g2"], 5)

            def by_head(i):
                return gates[:, 0:NV, i, :].rearrange("p v t -> p t v")

            dve.memset(gates[:, NV:], 0.0)
            dve.tensor_copy(by_head(0), G[:])
            ts(by_head(1), ga[:], -1.0, None, ALU.mult)
            dve.tensor_copy(by_head(2), gs[:])
            tt(by_head(3), gs[:], gc[:], ALU.mult)
            end()
            end()

            with dve.Fori(0, NH) as h:
                for b in range(B):
                    for i, qt in enumerate(SCORE_ORDER):
                        u = 4 * b + qt
                        dve.wait_ge(sm["s_sc"], 4 * b + max(i + 1, 2))
                        diag = score(b, qt)[:, qt * P:(qt + 1) * P]
                        tt(diag, diag, causal_neg[:], ALU.add).then_inc(sm["s_msk"], 1)
                        dve.wait_ge(sm["s_msk"], 4 * b + i + 1)
                        dve.tensor_reduce(nmax[:, u:u + 1], score(b, qt), AX.X, ALU.max).then_inc(sm["s_max"], 1)
                    dve.wait_ge(sm["s_max"], 4 * b + 4)
                    ts(bias[:, 4 * b:4 * b + 4], nmax[:, 4 * b:4 * b + 4], -ATT_SCALE, None,
                       ALU.mult).then_inc(sm["s_bias"], 1)
                for n in range(2):
                    dve.wait_ge(sm["s_v"], n + 1)
                    dve.tensor_copy(vt[:, 4 * n:4 * n + 4, :], ps[:, 6 + n, :].rearrange("p (t d) -> p t d", t=4))\
                       .then_inc(sm["s_vE"], 1)
                for b in range(B):
                    dve.wait_ge(sm["s_exp"], 4 * b + 4)
                    dve.reciprocal(prec[:, 4 * b:4 * b + 4], psums[:, 4 * b:4 * b + 4]).then_inc(sm["s_rec"], 1)
                    dve.wait_ge(sm["s_rec"], b + 1)
                    for qt in range(4):
                        u = 4 * b + qt
                        p_row = prob[:, u, 0:(qt + 1) * P]
                        ts(p_row, p_row, prec[:, u:u + 1], None, ALU.mult).then_inc(sm["s_prob"], 1)
                for n in range(4):
                    dve.wait_ge(sm["s_o"], n + 1)
                    rows = hid[:, 2 * n:2 * n + 2, :].rearrange("p t h -> p (t h)")
                    tt(rows, ps[:, n, :], rows, ALU.add).then_inc(sm["s_oE"], 1)
                end()

            dve.wait_ge(sm["s_rms"], 1)
            step(dve.reciprocal(rrms[:], rms[:]))
            for t in range(NT):
                ts(xr[:, t, :], hid[:, t, :], rrms[:, t:t + 1], None, ALU.mult).then_inc(sm["s_xr"], 1)
            tt(total[:], total[:], hid[:], ALU.add)
            dve.wait_ge(sm["s_ba"], 1)

            def over_experts(x):
                return x[:].unsqueeze(2).broadcast_to([P, NT, E])

            step(dve.tensor_copy(lg[:], ps[:, 4, 0:NT * E].rearrange("p (t e) -> p t e", t=NT)))
            step(dve.tensor_reduce(lmax[:], lg[:], AX.X, ALU.max))
            tt(lg[:], lg[:], over_experts(lmax), ALU.subtract).then_inc(sm["s_g1"], 1)
            dve.wait_ge(sm["s_g2"], 1)
            step(dve.tensor_reduce(lsum[:], lg[:], AX.X, ALU.add))
            step(dve.reciprocal(lrec[:], lsum[:]))
            step(tt(pr[:], lg[:], over_experts(lrec), ALU.mult))
            other = pr[:].unsqueeze(2).broadcast_to([P, NT, E, E])
            own = pr[:].unsqueeze(3).broadcast_to([P, NT, E, E])
            tt(cmp_a, other, own, ALU.is_gt)
            step(tt(cmp_b, other, own, ALU.is_equal))
            step(tt(cmp_b, cmp_b, before[:].unsqueeze(1).broadcast_to([P, NT, E, E]), ALU.mult))
            step(tt(cmp_a, cmp_a, cmp_b, ALU.add))
            step(dve.tensor_reduce(rank[:], cmp_a, AX.X, ALU.add))
            step(ts(keep[:], rank[:], TOPK - 0.5, None, ALU.is_lt))
            step(tt(keep[:], keep[:], pr[:], ALU.mult))
            step(dve.tensor_reduce(lsum[:], keep[:], AX.X, ALU.add))
            step(dve.reciprocal(lrec[:], lsum[:]))
            step(tt(wfull[:, :, 0:E], keep[:], over_experts(lrec), ALU.mult))
            step(dve.memset(wfull[:, :, E:E + 1], 1.0))
            left = [wfull[:], rest[:, 0], rest[:, 1]]
            for i in range(3):
                step(dve.tensor_copy(wh[:, :, i, :], left[i]))
                if i < 2:
                    step(dve.tensor_copy(ws[:, :, i, :], wh[:, :, i, :]))
                    step(tt(left[i + 1], left[i], ws[:, :, i, :], ALU.subtract))
                else:
                    dve.tensor_copy(ws[:, :, i, :], wh[:, :, i, :]).then_inc(sm["s_g"], 1)
            for n in range(2):
                dve.wait_ge(sm["s_grT"], n + 1)
                dve.tensor_copy(wT[:, n * 512:(n + 1) * 512], ps[0:3 * (E + 1), 5 + n, :])
            end()

            with dve.Fori(0, NG) as i:
                for u in range(2 * FG):
                    j, n = u // 2, u % 2
                    dve.wait_ge(sm["s_sg"], u + 1)
                    if u >= 2:
                        dve.wait_ge(sm["s_act"], u - 1)
                    tt(su[:, n, :], ps[:, 3 * n + 1, :], sg[:, n, :], ALU.mult).then_inc(sm["s_su"], 1)
                    dve.wait_ge(sm["s_su"], u + 1)
                    tt(act_t[:, j, n * 512:(n + 1) * 512], ps[:, 3 * n + 2, :], su[:, n, :],
                       ALU.mult).then_inc(sm["s_act"], 1)
                for t in range(NT):
                    dve.wait_ge(sm["s_dn"], t + 1)
                    tt(total[:, t, :], ps[:, 6 + t % 2, 0:H], total[:, t, :], ALU.add).then_inc(sm["s_dnE"], 1)
                end()

            def convolve(u, bank):
                i = (1, 0, 2, 3)[u // 2]
                for k in range(1, TAPS):
                    if k == 1:
                        dve.wait_ge(sm["s_tap"], u + 1)
                    else:
                        dve.wait_ge(sm["s_taps"], 2 * u + k - 1)
                    row = cv[:, u % 4, k:S]
                    stt(row, ps[:, bank, 0:S - k], cw[:, i, TAPS - 1 - k:TAPS - k], row, ALU.mult, ALU.add)\
                        .then_inc(sm["s_conv" if k == TAPS - 1 else "s_taps"], 1)

            def decay_exponents(nx, k=1):
                dve.wait_ge(sm["s_gm"], k)
                for r in range(R):
                    last = tt(dec[:, r], dec[:, r], gh[:, nx, r, 0, :].unsqueeze(2).broadcast_to([P, NT, CH]), ALU.subtract)
                last.then_inc(sm["s_gsub"], 1)
                dve.tensor_copy(eglast[:, nx], Ebc[:].rearrange("p r (a i) -> p r a i", i=CH)[:, :, :, CH - 1])\
                    .then_inc(sm["s_pre"], 1)

            kq = ps[:, 4:6, :].rearrange("p a (t m i) -> p (a t) m i", m=2, i=CH)

            def key_lengths(nx):
                dve.wait_ge(sm["s_kq"], 1)
                step(tt(diag_k[:], kq[:, :, 0, :], eye_c[:].unsqueeze(1).broadcast_to([P, NT, CH]), ALU.mult))
                dve.tensor_reduce(ss[:, 0, :], diag_k[:], AX.X, ALU.add).then_inc(sm["s_ssk"], 1)
                dve.wait_ge(sm["s_ssk"], 1)
                step(ts(rk2[:], ss[:, 0, :], 1e-6, None, ALU.add))
                step(dve.reciprocal(rk2[:], rk2[:]))
                step(tt(cb[:], gh[:, nx, :, 2:4, :], rk2[:].unsqueeze(1).unsqueeze(1).broadcast_to([P, R, 2, NT]), ALU.mult))

            def system(r):
                step(tt(dec[:, r], dec[:, r], cb[:, r, 0, :].unsqueeze(2).broadcast_to([P, NT, CH]), ALU.mult))
                for q in range(4):
                    rows, w = slice(q * BL, (q + 1) * BL), (q % 2) * BL
                    last = stt(MTc[rows, r], kq[rows, :, 0, w:w + BL], -1.0, dec[rows, r, :, w:w + BL], ALU.mult, ALU.mult)
                last.then_inc(sm["s_mt"], 1)

            def beside_and_attention(r):
                for q in (0, 2):
                    rows = slice(q * BL, (q + 1) * BL)
                    stt(MOFF[rows, r, :, (q + 1) * BL:(q + 2) * BL], kq[rows, :, 0, BL:2 * BL], -1.0,
                        dec[rows, r, :, BL:2 * BL], ALU.mult, ALU.mult)
                tt(BK[:, r, :, 0:CH], kq[:, :, 1, :], dec[:, r], ALU.mult).then_inc(sm["s_at"], 1)

            def decayed_keys(n, bank):
                dve.wait_ge(sm["s_kt"], n + 1)
                for r in range(R):
                    last = tt(BK[:, r, 4 * n:4 * n + 4, CH:], ps[:, bank, :].rearrange("p (t d) -> p t d", d=D),
                              cb[:, r, 1, 4 * n:4 * n + 4].unsqueeze(2).broadcast_to([P, 4, D]), ALU.mult)
                last.then_inc(sm["s_kd"], 1)

            def query_scale(nx):
                dve.wait_ge(sm["s_nrm"], 1)
                step(dve.reciprocal(rq[:, nx], nrm[:, 1, :]))
                step(ts(rq[:, nx], rq[:, nx], D ** -0.5, None, ALU.mult))

            def values(u, nx, bank):
                r, n = u // 2, u % 2
                dve.wait_ge(sm["s_vt"], u + 1)
                tt(vs[:, nx, r, 4 * n:4 * n + 4, :], ps[:, bank, :].rearrange("p (t d) -> p t d", d=D),
                   nrm[:, 0, 4 * n:4 * n + 4].unsqueeze(2).broadcast_to([P, 4, D]), ALU.mult).then_inc(sm["s_vTE"], 1)

            def solve_row(i):
                if i == 1:
                    step(dve.tensor_copy(Tb[:], eye16[:]))
                    dve.wait_ge(sm["s_blk"], 16 * 4)
                step(tt(Tprod[:, 0:i, 0:i], Tb[:, 0:i, 0:i].rearrange("p j c -> p c j"),
                        blk[:, 0:i, i].unsqueeze(1).broadcast_to([P, i, i]), ALU.mult))
                last = dve.tensor_reduce(Tb[:, i, 0:i], Tprod[:, 0:i, 0:i], AX.X, ALU.add)
                if i < SB - 1:
                    step(last)
                else:
                    last.then_inc(sm["s_solve"], 1)

            def transposed_blocks(r, s):
                for q in range(4):
                    rows = slice(q * BL, (q + 1) * BL)
                    last = dve.transpose(TTbd[rows, r, :, q * BL:(q + 1) * BL], Tc[rows, r])
                last.then_inc(sm[s], 1)

            def solved_blocks(r):
                dve.wait_ge(sm["s_tq"], 32)
                step(tt(Tc[:, r].rearrange("p t (w j) -> p t w j", w=2), Tq[:, r].unsqueeze(2).broadcast_to([P, NT, 2, SB]),
                        half[:].unsqueeze(1).unsqueeze(3).broadcast_to([P, NT, 2, SB]), ALU.mult))
                transposed_blocks(r, "s_tt")

            def blocks_of_32(r):
                dve.wait_ge(sm["s_pa"], r + 1)
                dve.copy_predicated(Tc[:, r].rearrange("p t c -> p (t c)"), m16[:], ps[:, 4 + r, 256:512])\
                    .then_inc(sm["s_paE"], 1)
                dve.wait_ge(sm["s_paE"], r + 1)
                transposed_blocks(r, "s_tt2")
                dve.wait_ge(sm["s_tt2"], r + 1)
                dve.transpose(T64[:, r].rearrange("p t c -> p (t c)"), TTbd[:, r].rearrange("p t c -> p (t c)"))\
                    .then_inc(sm["s_t64"], 1)

            def take_products(u, nx):
                r, m = u // 4, u % 4
                dve.wait_ge(sm["s_y"], u + 1)
                dve.tensor_copy(AW[:, nx, r, 2 * m:2 * m + 2, :],
                                ps[:, 6 + u % 2, 0:2 * (CH + D)].rearrange("p (t d) -> p t d", t=2)).then_inc(sm["s_yF"], 1)

            def output_scale(v):
                dve.wait_ge(sm["s_nrm"], v)
                step(dve.reciprocal(rr2[:], rms2[:]))

            def add_output(t):
                dve.wait_ge(sm["s_wo"], t + 1)
                for r in range(R):
                    if r:
                        dve.wait_ge(sm["s_wo1"], t + 1)
                    stt(total[:, t, :], ps[:, 4 + t % 2, r * H:(r + 1) * H], rr2[:, r, t:t + 1], total[:, t, :],
                        ALU.mult, ALU.add).then_inc(sm["s_woE" if r else "s_wo1"], 1)

            all_gates = gates[:].rearrange("p (k r) c t -> p k (r c t)", r=R)

            dve.wait_ge(sm["s_w"], 16 * 10)
            dve.wait_ge(sm["s_zero"], 3)
            step(dve.tensor_copy(gh[:, 0].rearrange("p r c t -> p (r c t)"), all_gates[:, 0, :]))
            decay_exponents(0)
            order = flow_order(True, False)

            def bank_in(order, x):
                return {"p0": 4, "p1": 5}[x] if x in ("p0", "p1") else 6 + order.index(x) % 2

            for u in range(4):
                convolve(u, bank_in(order, "p%d" % u))
            key_lengths(0)
            dve.wait_ge(sm["s_E"], 1)
            for r in range(R):
                system(r)
            for n in range(2):
                decayed_keys(n, bank_in(order, "k%d" % n))
            for r in range(R):
                beside_and_attention(r)
            for u in (4, 5, 6):
                convolve(u, bank_in(order, "p%d" % u))
            query_scale(0)
            for u in (0, 1):
                values(u, 0, bank_in(order, "v%d" % u))
            convolve(7, bank_in(order, "p7"))
            for u in (2, 3):
                values(u, 0, bank_in(order, "v%d" % u))
            for i in range(1, SB):
                solve_row(i)
            step(dve.tensor_copy(gh[:, 1].rearrange("p r c t -> p (r c t)"), all_gates[:, 1, :]))
            dve.wait_ge(sm["s_gl"], 16 * 6)
            decay_exponents(1, 2)
            for r in range(R):
                solved_blocks(r)
            for r in range(R):
                blocks_of_32(r)
            for u in range(1, 8, 2):
                take_products(u, 0)
            end()

            def gdn_body(i, par, last_body):
                nx = 1 - par
                order = flow_order(not last_body)

                def bank(x):
                    return bank_in(order, x)

                def residuals(n, b):
                    rows, t = slice((n % 2) * CH, (n % 2 + 1) * CH), 4 * b + n // 2
                    dve.wait_ge(sm["s_p1"], 2 * (n - 1) + b + 1)
                    for r in range(R):
                        last = stt(Rb[rows, b * R + r, :], ps[rows, b, r * D:(r + 1) * D], gh[rows, par, r, 1, t:t + 1],
                                   vs[rows, par, r, t, :], ALU.mult, ALU.add)
                    last.then_inc(sm["s_R"], 1)

                def states(n, b):
                    now = n % 2
                    dve.wait_ge(sm["s_p2"], 2 * n + b + 1)
                    new = ps[:, b, R * D:2 * R * D]
                    if n == 0:
                        last = dve.tensor_copy(St[:, 1, b * R:(b + 1) * R, :].rearrange("p r d -> p (r d)"), new)
                    else:
                        for r in range(R):
                            a = 2 * (4 * b + n // 2) + n % 2
                            last = stt(St[:, 1 - now, b * R + r, :], St[:, now, b * R + r, :], eglast[:, par, r, a:a + 1],
                                       new[:, r * D:(r + 1) * D], ALU.mult, ALU.add)
                    last.then_inc(sm["s_S"], 1)

                def gate(m):
                    dve.wait_ge(sm["s_zE"], m + 1)
                    if m >= 2:
                        dve.wait_ge(sm["s_x"], m - 1)
                        dve.wait_ge(sm["s_sqx"], 4 * (m - 1))
                    for b in range(B):
                        t = 4 * b + m
                        dve.wait_ge(sm["s_O"], 2 * (2 * m + 1) + b + 1)
                        for r in range(R):
                            last = stt(xo[:, m % 2, b * R + r, :], ps[:, 2 + b, r * D:(r + 1) * D], rq[:, par, t:t + 1],
                                       sz[:, m % 2, b, r * D:(r + 1) * D], ALU.mult, ALU.mult)
                        last.then_inc(sm["s_gate"], 1)

                def pre(f, *a):
                    if not last_body:
                        f(*a)

                def conv(*units):
                    for u in units:
                        if not last_body:
                            convolve(u, bank("p%d" % u))

                def solve_rows(a, b):
                    for k in range(a, b):
                        pre(solve_row, k)

                for n in range(STEPS):
                    if n:
                        for b in range(B):
                            residuals(n, b)
                    if n == 0:
                        conv(0)
                    if n == 1:
                        conv(3)
                    if n and n % 2 == 0:
                        gate(n // 2 - 1)
                    if n == 3:
                        for r in range(R):
                            pre(beside_and_attention, r)
                    if n == 5:
                        pre(query_scale, nx)
                        pre(values, 0, nx, bank("v0") if not last_body else 0)
                    if n < STEPS - 1:
                        for b in range(B):
                            states(n, b)
                    if n == 0:
                        conv(1, 2)
                    if n == 2:
                        pre(key_lengths, nx)
                        for r in range(R):
                            pre(system, r)
                        for k in range(2):
                            pre(decayed_keys, k, bank("k%d" % k) if not last_body else 0)
                    if n == 3:
                        conv(4, 5)
                        solve_rows(1, 5)
                    if n == 4:
                        conv(6)
                        solve_rows(5, 10)
                    if n == 5:
                        pre(values, 1, nx, bank("v1") if not last_body else 0)
                        solve_rows(10, SB)
                        conv(7)
                    if n == 6:
                        output_scale(1 if last_body else 2)
                        for t in range(4):
                            add_output(t)
                        for u in (2, 3):
                            pre(values, u, nx, bank("v%d" % u) if not last_body else 0)
                        for t in range(4, NT):
                            add_output(t)
                if not last_body:
                    h = 2 * i + par + 2
                    src = all_gates[:, h, :] if isinstance(i, int) else all_gates[:, bass.ds(i * 2 + (par + 2), 1), :].squeeze(1)
                    dve.wait_ge(sm["s_gl"], 48)
                    dve.wait_ge(sm["s_R"], 2 * (STEPS - 1))
                    dve.wait_ge(sm["s_S"], 2 * (STEPS - 1))
                    step(dve.tensor_copy(gh[:, par].rearrange("p r c t -> p (r c t)"), src))
                    decay_exponents(par)
                    for r in range(R):
                        solved_blocks(r)
                gate(3)
                if not last_body:
                    for r in range(R):
                        blocks_of_32(r)
                    for u in range(1, 8, 2):
                        take_products(u, nx)
                end()

            gdn_bodies(dve, gdn_body)
            output_scale(1)
            for t in range(NT):
                add_output(t)
            end()

        @block.gpsimd
        def _(pool):
            pool.memset(eps5[:], 1e-5).then_inc(sm["s_eps"], 1)
            pool.memset(eps6[:], 1e-6).then_inc(sm["s_eps"], 1)
            pool.wait_ge(sm["s_xn"], NT)
            pool.tensor_copy(hid[:], xn[:])
            section_end(pool, "pool")
            section_end(pool, "pool")
            with pool.Fori(0, NH) as h:
                section_end(pool, "pool")
            section_end(pool, "pool")
            with pool.Fori(0, NG) as i:
                section_end(pool, "pool")
            tt = pool.tensor_tensor

            def mask_decays():
                for r in range(R):
                    last = tt(dec[:, r], Gbc[:, r], e_neg[:].unsqueeze(1).broadcast_to([P, NT, CH]), ALU.add)
                last.then_inc(sm["s_gm"], 1)

            def prepare(nx):
                pool.wait_ge(sm["s_silu"], 4)
                for r in range(R):
                    tt(qg[:, nx, r], qT[:], Ebc[:, r], ALU.mult).then_inc(sm["s_qg"], 1)
                pool.wait_ge(sm["s_qg"], R)
                for i, q in enumerate((1, 3)):
                    pool.memset(MTbd[q * BL:(q + 1) * BL, :, :, (q - 1) * BL:q * BL], 0.0).then_inc(sm["s_rezero"], 1)
                    pool.wait_ge(sm["s_rezero"], i + 1)
                for r in range(R):
                    pool.wait_ge(sm["s_mt"], r + 1)
                    for q in range(4):
                        rows = slice(q * BL, (q + 1) * BL)
                        if r or q:
                            pool.wait_ge(sm["s_bd"], 4 * r + q)
                        pool.tensor_copy(MTbd[rows, r, :, q * BL:(q + 1) * BL], MTc[rows, r]).then_inc(sm["s_bd"], 1)
                pool.wait_ge(sm["s_bd"], 4 * R)

            pool.wait_ge(sm["s_w"], 16 * 10)
            pool.wait_ge(sm["s_gl"], 16 * 3)
            mask_decays()
            for x in (MTbd, MOFF, TTbd):
                pool.memset(x[:], 0.0).then_inc(sm["s_zero"], 1)
            for x in (xT[:, 1], ss2[:, 1]):
                pool.memset(x, 0.0)
            pool.wait_ge(sm["s_zero"], 3)
            prepare(0)
            pool.wait_ge(sm["s_gl"], 16 * 6)
            pool.wait_ge(sm["s_at"], R)
            mask_decays()
            section_end(pool, "pool")

            def gdn_body(i, par, last_body):
                if not last_body:
                    prepare(1 - par)
                    pool.wait_ge(sm["s_gl"], 48)
                    pool.wait_ge(sm["s_at"], R)
                    mask_decays()
                section_end(pool, "pool")

            gdn_bodies(pool, gdn_body)
            section_end(pool, "pool")


_OUT = (2, 512, 256)


def layout(x):
    import numpy as np
    c = np.ascontiguousarray

    def halves(a):
        return a.reshape(HK, P, -1).transpose(1, 0, 2)

    def wrap(a, n=1):
        return np.concatenate([a, a[:n]])

    qw = x["L0_ffn_q_w"].reshape(NH, 192, H)[:, :P]
    kvw = x["L0_ffn_kv_w"]
    kw, vw = kvw[:NH * P].reshape(NH, P, H), kvw[NH * P:2 * NH * P].reshape(NH, P, H)
    o = {"x": x["L0_attn_hidden_states"].reshape(TOK, H)}
    o["wqk"] = wrap(np.concatenate([qw, kw], 1).reshape(NH, 2 * P, HK, P).transpose(0, 3, 2, 1), 2)
    o["wv"] = wrap(vw.reshape(NH, P, HK, P).transpose(0, 3, 2, 1))
    o["wo"] = wrap(x["L0_ffn_o_w"].T.reshape(NH, P, H))
    o["ln1"] = x["L0_ffn_ln1_w"].reshape(HK, P).T
    o["ln2"] = x["L0_ffn_ln2_w"].reshape(HK, P).T
    o["wgate"] = halves(x["L0_ffn_gate_w"].T)
    pad = np.zeros((FT * P - E * I - SHI, H), np.float32)
    w1, sh = x["L0_ffn_w1"], x["L0_ffn_sh_gu_w"]
    gate_rows = np.concatenate([w1[:, :I].reshape(E * I, H), sh[:SHI], pad])
    up_rows = np.concatenate([w1[:, I:].reshape(E * I, H), sh[SHI:], pad])
    gu = np.concatenate([gate_rows.reshape(FT, P, H), up_rows.reshape(FT, P, H)], 1)
    gu = gu.reshape(NG, FG, 2 * P, HK, P).transpose(0, 4, 1, 3, 2)
    o["w13"] = wrap(gu)
    dn = np.concatenate([x["L0_ffn_w2"].transpose(0, 2, 1).reshape(E * I, H), x["L0_ffn_sh_down_w"].T, pad])
    o["w2"] = wrap(dn.reshape(NG, FG, P, H).transpose(0, 2, 1, 3))
    wba = x["L0_attn_W_ba"].reshape(H, NK, 2, R)
    o["wba"] = halves(wba.transpose(0, 2, 1, 3).reshape(H, 2 * NV))
    o["alog"], o["dtb"] = x["L0_attn_A_log"], x["L0_attn_dt_bias"]
    w = x["L0_attn_W_qkvz"].reshape(HK, P, NK, 4 * D + R * D).transpose(2, 1, 0, 3)
    o["wA"] = wrap(w[..., :4 * D], 2)
    o["wz"] = wrap(w[..., 4 * D:])
    cwt = x["L0_attn_conv_weight"]
    qc, kc, vc = (cwt[a:b].reshape(NK, -1, P, TAPS) for a, b in
                  ((0, NK * D), (NK * D, 2 * NK * D), (2 * NK * D, 2 * NK * D + NV * D)))
    o["cw"] = wrap(np.concatenate([qc, kc, vc], 1).transpose(0, 2, 1, 3), 2)
    wout = x["L0_attn_W_out"].reshape(NK, R, D, H).transpose(0, 2, 1, 3)
    o["wout"] = np.concatenate([wout[-1:], wout])
    o["normw"] = x["L0_attn_norm_weight"].reshape(D, 1)
    return {n: c(a) for n, a in o.items()} | constants()


def constants():
    import numpy as np
    from concourse import mybir as mb
    i = np.arange(P)
    same = i[:, None] // CH == i[None] // CH
    rows = np.minimum(np.arange(FT * P) // I, E)
    sel = (rows[None] == np.arange(E + 1)[:, None]).astype(np.float32)
    sel = np.tile(sel, (3, 1)).reshape(3 * (E + 1), NG, FG * P).transpose(1, 0, 2)
    e = np.arange(E)
    row, col = i[:, None] % BL, np.arange(BL)[None]
    m16 = np.tile(((row >= SB) & (col < SB)).astype(np.int32), (1, NT))
    src, dst = i[:, None] % CH, np.arange(CH)[None]
    return {
        "e_neg": np.where(src <= dst, 0.0, NEG).astype(np.float32),
        "eye_c": (src == dst).astype(np.float32),
        "eye16": np.tile(np.eye(SB, dtype=np.float32), (P, 1, 1)),
        "m16": m16,
        "half": (row // SB == np.arange(2)[None]).astype(np.float32),
        "ident": np.eye(P, dtype=np.float32),
        "cum_mask": (same & (i[:, None] <= i[None])).astype(np.float32),
        "chunk_ones": same.astype(np.float32),
        "causal_neg": np.where(i[None] <= i[:, None], 0.0, NEG).astype(np.float32),
        "before": np.tile((e[None] < e[:, None]).astype(np.float32), (P, 1, 1)),
        "sel": np.ascontiguousarray(np.concatenate([sel, sel[:1]])).astype(mb.dt.np(BF16)),
    }


def kernel(**inputs):
    import numpy as np
    import concourse.bacc as bacc
    from concourse.bass_utils import run_bass_kernel_spmd

    nc = bacc.Bacc("TRN2", target_bir_lowering=False, num_devices=1)
    arrays, d = {}, {}
    for name, a in layout({k: np.asarray(v) for k, v in inputs.items()}).items():
        arrays["in_" + name] = a
        d[name] = nc.dram_tensor("in_" + name, a.shape, mybir.dt.from_np(a.dtype), kind="ExternalInput").ap()
    out = nc.dram_tensor("out_0", [TOK, H], F32, kind="ExternalOutput").ap()
    build(nc, d, out)
    r = run_bass_kernel_spmd(nc, [arrays], core_ids=[0])
    return r.results[0]["out_0"].reshape(_OUT)
```

```python
from contextlib import ExitStack

import concourse.bass as bass
from concourse import mybir

P = 128
B, S, H = 2, 512, 256
TOK = B * S
NT = TOK // P
HK = H // P
NK, NV, D = 16, 32, 128
R = NV // NK
CH = 64
TAPS = 4
BL = 32
SB = 16
NC = B * R
STEPS = S // CH
NH = 16
ATT_SCALE = (128 + 64) ** -0.5
E, I, TOPK, SHI = 16, 176, 4, 352
FT = 25
FG = 5
NG = FT // FG
NEG = -1.0e30
AU = 4
SCORE_ORDER = (0, 2, 1, 3)

F32 = mybir.dt.float32
BF16 = mybir.dt.bfloat16
ALU = mybir.AluOpType
ACT = mybir.ActivationFunctionType
AX = mybir.AxisListType


def build(nc, d, out, debug=None):
    grow_dram = nc.dram_tensor("grow_dram", [NV + 2 * R, TOK], F32).ap()
    erow_dram = nc.dram_tensor("erow_dram", [NV + 2 * R, TOK], F32).ap()
    mt_dram = nc.dram_tensor("mt_dram", [R, NT, P, BL], F32).ap()
    tb_dram = nc.dram_tensor("tb_dram", [R, NT, 4, 2, SB * SB], F32).ap()

    with ExitStack() as ctx:
        def sb(name, shape, dt=F32):
            return ctx.enter_context(nc.sbuf_tensor(name, shape, dt))

        def sem(name):
            return ctx.enter_context(nc.semaphore(name))

        ps = ctx.enter_context(nc.psum_tensor("ps", [P, 8, 512], F32))

        ident = sb("ident", [P, P])
        total = sb("total", [P, NT, H])
        xnT = sb("xnT", [P, HK, TOK])
        gates = sb("gates", [P, NV + R, 4, NT])
        eps6 = sb("eps6", [P, 1])

        early_ctx = ExitStack()

        def early(name, shape, dt=F32):
            return early_ctx.enter_context(nc.sbuf_tensor(name, shape, dt))

        cum_mask = early("cum_mask", [P, P])
        chunk_ones = early("chunk_ones", [P, P])
        causal_neg = early("causal_neg", [P, P])
        ln1 = early("ln1", [P, HK])
        ln2 = early("ln2", [P, HK])
        xn = early("xn", [P, NT, H])
        hid = early("hid", [P, NT, H])
        xrT = early("xrT", [P, HK, TOK])
        wba = early("wba", [P, HK, 2 * NV])
        alog = early("alog", [P, NV])
        dtb = early("dtb", [P, NV])
        stats = early("stats", [P, NT, 6])
        mv = early("mv", [P, NT, 2])
        sd = early("sd", [P, NT])
        rstd = early("rstd", [P, NT])
        ssq = early("ssq", [P, NT])
        rms = early("rms", [P, NT])
        rrms = early("rrms", [P, NT])
        junk = early("junk", [P, H])
        eps5 = early("eps5", [P, 1])
        ba = early("ba", [P, NT, 2 * NV])
        ga = early("ga", [P, NT, NV])
        gb = early("gb", [P, NT, NV])
        gc = early("gc", [P, NT, NV])
        gs = early("gs", [P, NT, NV])
        g = early("g", [P, NT, NV])
        G = early("G", [P, NT, NV])
        growT = early("growT", [NV, TOK])
        erowT = early("erowT", [NV, TOK])
        wqk = early("wqk", [P, HK, 2 * P])
        wv = early("wv", [P, HK, P])
        wo = early("wo", [P, H])
        aqT = early("aqT", [P, TOK])
        akT = early("akT", [P, TOK])
        vt = early("vt", [P, NT, P])
        prob = early("prob", [P, NT, 4 * P])
        probT = early("probT", [P, NT, 4 * P])
        nmax = early("nmax", [P, NT])
        bias = early("bias", [P, NT])
        psums = early("psums", [P, NT])
        prec = early("prec", [P, NT])
        attT = early("attT", [P, TOK])
        wgate = early("wgate", [P, HK, E])
        lg = early("lg", [P, NT, E])
        lmax = early("lmax", [P, NT])
        lsum = early("lsum", [P, NT])
        lrec = early("lrec", [P, NT])
        pr = early("pr", [P, NT, E])
        before = early("before", [P, E, E])
        rank = early("rank", [P, NT, E])
        keep = early("keep", [P, NT, E])
        wfull = early("wfull", [P, NT, E + 1])
        rest = early("rest", [P, 2, NT, E + 1])
        ws = early("ws", [P, NT, 3, E + 1])
        wh = early("wh", [P, NT, 3, E + 1], BF16)
        wT = early("wT", [3 * (E + 1), TOK], BF16)
        sel = early("sel", [3 * (E + 1), FG * P], BF16)
        w13 = early("w13", [P, FG, HK, 2 * P])
        w2 = early("w2", [P, FG, H])
        sg = early("sg", [P, 2, 512])
        su = early("su", [P, 2, 512])
        act_t = early("act_t", [P, FG, TOK])
        xr = prob[:, :, 0:H]
        cmp_a = act_t[:, 0:2, :].rearrange("p a (t e f) -> p (a t) e f", e=E, f=E)
        cmp_b = act_t[:, 2:4, :].rearrange("p a (t e f) -> p (a t) e f", e=E, f=E)

        def score(b, qt):
            bank, at = ((3 * b, 0), (3 * b + 1, 0), (3 * b, P), (3 * b + 2, 0))[qt]
            return ps[:, bank, at:at + (qt + 1) * P]
        early_ctx.close()

        wA = sb("wA", [P, HK, 4 * P])
        wz = sb("wz", [P, HK, R * D])
        wout = sb("wout", [P, R, H])
        cw = sb("cw", [P, 4, TAPS])
        normw = sb("normw", [P, 1])
        cv = sb("cv", [P, 4, S])
        kT = sb("kT", [P, 2, TOK])
        qT = sb("qT", [P, TOK])
        vT = sb("vT", [P, 2, S])
        sz = sb("sz", [P, 2, B, R * D])
        junk_x = sb("junk_x", [P, NC, D])
        gh = sb("gh", [P, 2, R, 4, NT])
        Gbc = sb("Gbc", [P, R, NT, CH])
        Ebc = sb("Ebc", [P, R, TOK])
        eglast = sb("eglast", [P, 2, R, NT * 2])
        dec = sb("dec", [P, R, NT, CH])
        e_neg = sb("e_neg", [P, CH])
        eye_c = sb("eye_c", [P, CH])
        diag_k = sb("diag_k", [P, NT, CH])
        ss = sb("ss", [P, 2, NT])
        nrm = sb("nrm", [P, 2, NT])
        rk2 = sb("rk2", [P, NT])
        rq = sb("rq", [P, 2, NT])
        cb = sb("cb", [P, R, 2, NT])
        qg = sb("qg", [P, 2, R, TOK])
        MTc = sb("MTc", [P, R, NT, BL])
        MTbd = sb("MTbd", [P, R, NT, P])
        T64 = MTbd
        MOFF = sb("MOFF", [P, R, NT, P])
        blk = sb("blk", [P, SB, SB])
        Tb = sb("Tb", [P, SB, SB])
        Tprod = sb("Tprod", [P, SB, SB])
        eye16 = sb("eye16", [P, SB, SB])
        m16 = sb("m16", [P, NT * BL], mybir.dt.int32)
        half = sb("half", [P, 2])
        Tq = sb("Tq", [P, R, NT, SB])
        Tc = sb("Tc", [P, R, NT, BL])
        Xc = MTc
        TTbd = sb("TTbd", [P, R, NT, P])
        BK = sb("BK", [P, R, NT, CH + D])
        AW = sb("AW", [P, 2, R, NT, CH + D])
        vs = sb("vs", [P, 2, R, NT, D])
        St = sb("St", [P, 2, NC, D])
        Rb = sb("Rb", [P, NC, D])
        xo = sb("xo", [P, 2, NC, D])
        xT = sb("xT", [P, 2, R, TOK])
        ss2 = sb("ss2", [P, 2, R, NT])
        rms2 = sb("rms2", [P, R, NT])
        rr2 = sb("rr2", [P, R, NT])

        names = ["s_const", "s_x", "s_stat", "s_sd", "s_rstd", "s_xn", "s_ssq", "s_rms", "s_rrms", "s_xr",
                 "s_tr", "s_trE", "s_ba", "s_baE", "s_g1", "s_g2", "s_g3", "s_dch", "s_g", "s_cum", "s_G", "s_grT",
                 "s_grE", "s_st", "s_eps",
                 "s_w", "s_qk", "s_qkE", "s_v", "s_vE", "s_sc", "s_msk", "s_max", "s_bias", "s_exp", "s_rec",
                 "s_prob", "s_pT", "s_pTE", "s_pv", "s_pvE", "s_o", "s_oE", "s_ld", "s_ldv", "s_ldq", "s_ldo",
                 "s_gu", "s_sg", "s_su", "s_act", "s_dn", "s_dnE",
                 "s_A", "s_raw", "s_vconv", "s_vtaps", "s_cb", "s_ovs", "s_tap", "s_taps", "s_conv", "s_silu", "s_gm", "s_gsub", "s_E", "s_gl", "s_pre", "s_kq", "s_ssk",
                 "s_kt", "s_kd", "s_qt", "s_sqq", "s_vt", "s_vTE", "s_nrm", "s_rr", "s_mt", "s_mtst", "s_blk", "s_solve",
                 "s_tbst", "s_tq", "s_at", "s_bd", "s_z", "s_zE", "s_qg", "s_tt", "s_xa", "s_xaE", "s_pa", "s_paE",
                 "s_tt2", "s_t64", "s_xb", "s_xbE", "s_pb", "s_pbE", "s_y", "s_yE", "s_yF", "s_p1", "s_R", "s_p2", "s_S", "s_O",
                 "s_gate", "s_sqx", "s_x2", "s_xE", "s_zero", "s_rezero", "s_wo", "s_wo1", "s_woE",
                 "s_end"]
        sm = {n: sem(n) for n in names}
        s_first, s_last = sm[names[0]].num, sm[names[-1]].num
        assert s_last - s_first == len(names) - 1
        go = {n: sem("go_" + n) for n in ("pe", "act", "dve", "pool")}

        def section_end(eng, who):
            eng.drain().then_inc(sm["s_end"], 1)
            eng.wait_ge(go[who], 1)
            eng.sem_clear(go[who])

        def section_end_sync(sp, dmas):
            for s, v in dmas:
                sp.wait_ge(sm[s], v)
            sp.wait_ge(sm["s_end"], 4)
            sp.sem_clear(range(s_first, s_last + 1))
            for who in go:
                sp.sem_inc(go[who], 1)

        def gdn_bodies(eng, body):
            with eng.Fori(0, NK // 2 - 1) as i:
                body(i, 0, False)
                body(i, 1, False)
            body(NK // 2 - 1, 0, False)
            body(NK // 2 - 1, 1, True)

        def output_bank(t):
            return t % 2 + (4 if t < 4 else 0)

        def flow_order(prepares, scans=True):
            order = ("p2 p3 z0 q0 q1 k0 k1 x0 p4 p5 z1 x1 z2 x2 z3 v0 v1 p6 p7 x3 v2 v3 y0 y1 y2 y3 y4 y5 y6 y7").split()
            return [x for x in order if (scans if x[0] in "zx" else prepares)]

        block = ctx.enter_context(nc.Block())

        @block.sync
        def _(sp):
            dma = sp.dma_start
            xv = d["x"].rearrange("(t p) h -> p t h", p=P)
            for i in range(2):
                dma(total[:, 4 * i:4 * i + 4, :], xv[:, 4 * i:4 * i + 4, :]).then_inc(sm["s_x"], 16)
            consts = [(ident, "ident"), (wba, "wba"), (alog, None), (dtb, None), (cum_mask, "cum_mask"),
                      (chunk_ones, "chunk_ones"), (ln1, "ln1"), (ln2, "ln2"), (causal_neg, "causal_neg"),
                      (wgate, "wgate"), (before, "before")]
            for t, n in consts:
                src = d[n] if n else {"alog": d["alog"], "dtb": d["dtb"]}[t.name].partition_broadcast(P)
                dma(t[:], src).then_inc(sm["s_const"], 16)
            for t, n in ((wqk, "wqk"), (wv, "wv"), (wo, "wo"), (w13, "w13"), (w2, "w2"), (sel, "sel")):
                dma(t[:], d[n][0]).then_inc(sm["s_w"], 16)
            sp.wait_ge(sm["s_grE"], 2)
            for rows, table in ((grow_dram, growT), (erow_dram, erowT)):
                dma(rows[0:NV], table[:]).then_inc(sm["s_st"], 16)
                dma(rows[NV:NV + 2 * R], table[0:2 * R]).then_inc(sm["s_st"], 16)
            section_end_sync(sp, [("s_const", 16 * len(consts)), ("s_x", 32), ("s_w", 96), ("s_st", 64)])
            sp.wait_ge(sm["s_qk"], 4)
            dma(wqk[:], d["wqk"][1]).then_inc(sm["s_ld"], 16)
            section_end_sync(sp, [("s_ld", 16)])
            with sp.Fori(0, NH // AU) as i:
                for k in range(AU):
                    nxt, after = bass.ds(i * AU + (k + 1), 1), bass.ds(i * AU + (k + 2), 1)
                    sp.wait_ge(sm["s_v"], 2 * k + 2)
                    dma(wv[:], d["wv"][nxt]).then_inc(sm["s_ldv"], 16)
                    sp.wait_ge(sm["s_qk"], 4 * k + 4)
                    dma(wqk[:], d["wqk"][after]).then_inc(sm["s_ldq"], 16)
                    sp.wait_ge(sm["s_o"], 4 * k + 4)
                    dma(wo[:], d["wo"][nxt]).then_inc(sm["s_ldo"], 16)
                section_end_sync(sp, [("s_ldv", 16 * AU), ("s_ldq", 16 * AU), ("s_ldo", 16 * AU)])
            section_end_sync(sp, [])
            with sp.Fori(0, NG) as i:
                for j in range(FG):
                    sp.wait_ge(sm["s_gu"], 2 * j + 2)
                    dma(w13[:, j], d["w13"][1:][bass.ds(i, 1), :, j]).then_inc(sm["s_ld"], 16)
                sp.wait_ge(sm["s_dn"], NT)
                dma(sel[:], d["sel"][1:][bass.ds(i, 1)]).then_inc(sm["s_ld"], 16)
                dma(w2[:], d["w2"][1:][bass.ds(i, 1)]).then_inc(sm["s_ld"], 16)
                section_end_sync(sp, [("s_ld", 16 * (FG + 2))])
            first = ((wA, "wA"), (cw, "cw"), (e_neg, "e_neg"), (wz, "wz"), (normw, "normw"), (wout, "wout"),
                     (eye_c, "eye_c"), (eye16, "eye16"), (m16, "m16"), (half, "half"))
            for t, n in first:
                dma(t[:], d[n][0] if n in ("wA", "cw", "wz", "wout") else d[n]).then_inc(sm["s_w"], 16)

            def decays_of(h):
                rows = grow_dram.rearrange("(k r) (t c i) -> k c r t i", r=R, c=2, i=CH)
                for c in range(2):
                    src = rows[h, c] if isinstance(h, int) else rows[h, c].squeeze(0)
                    dma(Gbc[c * CH:(c + 1) * CH], src.partition_broadcast(CH)).then_inc(sm["s_gl"], 16)

            def exponentials_of(h):
                rows = erow_dram.rearrange("(k r) n -> k r n", r=R)
                src = rows[h] if isinstance(h, int) else rows[h].squeeze(0)
                dma(Ebc[:], src.partition_broadcast(P)).then_inc(sm["s_gl"], 16)

            decays_of(0)
            exponentials_of(0)

            def blocks_out_and_back():
                for r in range(R):
                    sp.wait_ge(sm["s_mt"], r + 1)
                    dma(mt_dram[r].rearrange("t p i -> p t i"), MTc[:, r]).then_inc(sm["s_mtst"], 16)
                sp.wait_ge(sm["s_mtst"], 16 * R)
                for r in range(R):
                    for s in range(2):
                        src = mt_dram[r].rearrange("t (q s j) (w i) -> s w (t q) j i", s=2, j=SB, w=2)[s, s]
                        dma(blk[r * 64 + s * 32:r * 64 + (s + 1) * 32], src).then_inc(sm["s_blk"], 16)
                sp.wait_ge(sm["s_solve"], 1)
                for r in range(R):
                    for s in range(2):
                        dma(tb_dram[r].rearrange("t q s x -> s (t q) x")[s],
                            Tb[r * 64 + s * 32:r * 64 + (s + 1) * 32].rearrange("p i j -> p (i j)")).then_inc(sm["s_tbst"], 16)
                sp.wait_ge(sm["s_tbst"], 16 * 2 * R)
                for r in range(R):
                    dma(Tq[:, r], tb_dram[r].rearrange("t q s (i j) -> (q s i) t j", j=SB)).then_inc(sm["s_tq"], 16)

            def ahead(slot, new_z):
                sp.wait_ge(sm["s_A"], 8)
                dma(wA[:], d["wA"][slot(2)]).then_inc(sm["s_ld"], 16)
                sp.wait_ge(sm["s_conv"], 4)
                sp.wait_ge(sm["s_vconv"], 4)
                dma(cw[:], d["cw"][slot(2)]).then_inc(sm["s_ld"], 16)
                if new_z:
                    sp.wait_ge(sm["s_z"], 4)
                    dma(wz[:], d["wz"][slot(1)]).then_inc(sm["s_ld"], 16)
                    sp.wait_ge(sm["s_wo"], NT)
                    dma(wout[:], d["wout"][slot(1)]).then_inc(sm["s_ld"], 16)

            sp.wait_ge(sm["s_gm"], 1)
            decays_of(1)
            sp.wait_ge(sm["s_qg"], R)
            sp.wait_ge(sm["s_pre"], 1)
            exponentials_of(1)
            blocks_out_and_back()
            ahead(lambda n: n - 1, False)
            section_end_sync(sp, [("s_w", 16 * len(first)), ("s_gl", 16 * 6), ("s_ld", 32), ("s_blk", 64), ("s_tq", 32)])

            def gdn_body(i, par, last):
                if not last:
                    def slot(n):
                        return 2 * i + par + n if isinstance(i, int) else bass.ds(i * 2 + (par + n), 1)

                    decays_of(slot(2))
                    sp.wait_ge(sm["s_qg"], R)
                    exponentials_of(slot(2))
                    blocks_out_and_back()
                    ahead(slot, True)
                    section_end_sync(sp, [("s_gl", 48), ("s_ld", 64), ("s_blk", 64), ("s_tq", 32)])
                else:
                    sp.wait_ge(sm["s_wo"], NT)
                    dma(wout[:], d["wout"][NK]).then_inc(sm["s_ld"], 16)
                    section_end_sync(sp, [("s_ld", 16)])

            gdn_bodies(sp, gdn_body)
            section_end_sync(sp, [])
            dma(out.rearrange("(t p) h -> p t h", p=P), total[:]).then_inc(sm["s_st"], 16)
            sp.wait_ge(sm["s_st"], 16)

        @block.tensor
        def _(pe):
            mm = pe.matmul

            pe.wait_ge(sm["s_const"], 16 * 11)
            for src, sname, base in ((xn, "s_xn", 0), (xr, "s_xr", 4)):
                for k in range(HK):
                    for n in range(2):
                        pe.wait_ge(sm[sname], 4 * n + 4)
                        for i in range(4):
                            last = pe.transpose(ps[:, base + 2 * k + n, i * P:(i + 1) * P],
                                                src[:, 4 * n + i, k * P:(k + 1) * P], ident[:])
                        last.then_inc(sm["s_tr"], 1)
            pe.wait_ge(sm["s_trE"], 8)
            for t in range(NT):
                for k in range(HK):
                    last = mm(ps[:, 0, t * 2 * NV:(t + 1) * 2 * NV], xnT[:, k, t * P:(t + 1) * P], wba[:, k, :],
                              start=(k == 0), stop=(k == HK - 1))
            last.then_inc(sm["s_ba"], 1)
            pe.wait_ge(sm["s_g"], 1)
            g_all = g[:].rearrange("p t v -> p (t v)")
            mm(ps[:, 1, 0:NT * NV], cum_mask[:], g_all, start=True, stop=True).then_inc(sm["s_cum"], 1)
            mm(ps[:, 2, 0:NT * NV], chunk_ones[:], g_all, start=True, stop=True).then_inc(sm["s_cum"], 1)
            pe.wait_ge(sm["s_G"], 1)
            for t in range(NT):
                last = pe.transpose(ps[0:NV, 3 + t // 4, (t % 4) * P:(t % 4 + 1) * P], G[:, t, :], ident[:])
                if t % 4 == 3:
                    last.then_inc(sm["s_grT"], 1)
            section_end(pe, "pe")

            def project_qk(k=0):
                if k:
                    pe.wait_ge(sm["s_ldq"], 16 * k)
                for j in range(4):
                    w, n = j // 2, j % 2
                    if j >= 2:
                        pe.wait_ge(sm["s_qkE"], 4 * k + j - 1)
                    for c in range(HK):
                        last = mm(ps[:, 6 + j % 2, :], wqk[:, c, w * P:(w + 1) * P], xrT[:, c, n * 512:(n + 1) * 512],
                                  start=(c == 0), stop=(c == HK - 1))
                    last.then_inc(sm["s_qk"], 1)

            project_qk()
            section_end(pe, "pe")

            def scores(k, b):
                for qt in SCORE_ORDER:
                    if k and b and qt in (1, 3):
                        pe.wait_ge(sm["s_oE"], 4 * (k - 1) + qt // 2 + 1)
                    q = (4 * b + qt) * P
                    mm(score(b, qt), aqT[:, q:q + P], akT[:, b * S:b * S + (qt + 1) * P],
                       start=True, stop=True).then_inc(sm["s_sc"], 1)

            with pe.Fori(0, NH // AU) as i:
                scores(0, 0)
                scores(0, 1)
                for k in range(AU):
                    if k:
                        pe.wait_ge(sm["s_ldv"], 16 * k)
                    for n in range(2):
                        if k:
                            pe.wait_ge(sm["s_oE"], 4 * (k - 1) + 3 + n)
                        for t in range(4 * n, 4 * n + 4):
                            for c in range(HK):
                                last = mm(ps[:, 6 + n, (t % 4) * P:(t % 4 + 1) * P], xrT[:, c, t * P:(t + 1) * P],
                                          wv[:, c, :], start=(c == 0), stop=(c == HK - 1))
                        last.then_inc(sm["s_v"], 1)
                    pe.wait_ge(sm["s_vE"], 2 * k + 2)
                    project_qk(k)
                    for b in range(B):
                        u = 8 * k + 4 * b
                        pe.wait_ge(sm["s_exp"], u + 4)
                        pe.wait_ge(sm["s_prob"], u + 4)
                        for kt in range(4):
                            if kt == 3:
                                pe.wait_ge(sm["s_pTE"], u + 1)
                            for qt in range(kt, 4):
                                last = pe.transpose(ps[:, 3 * b + kt % 3, qt * P:(qt + 1) * P],
                                                    prob[:, 4 * b + qt, kt * P:(kt + 1) * P], ident[:])
                            last.then_inc(sm["s_pT"], 1)
                    pe.wait_ge(sm["s_qkE"], 4 * k + 4)
                    for b in range(B):
                        for kt in range(4):
                            pe.wait_ge(sm["s_pTE"], 8 * k + 4 * b + kt + 1)
                            last = mm(ps[:, 6 + b, kt * P:S], vt[:, 4 * b + kt, :], probT[:, 4 * b + kt, kt * P:S],
                                      start=(kt == 0), stop=(kt == 3), skip_group_check=True)
                        last.then_inc(sm["s_pv"], 1)
                    if k < AU - 1:
                        scores(k + 1, 0)
                    if k:
                        pe.wait_ge(sm["s_ldo"], 16 * k)
                    for t in range(NT):
                        if t % 4 == 0:
                            pe.wait_ge(sm["s_pvE"], 2 * k + t // 4 + 1)
                        last = mm(ps[:, 4 + t // 2, (t % 2) * H:(t % 2 + 1) * H], attT[:, t * P:(t + 1) * P], wo[:],
                                  start=True, stop=True)
                        if t % 2:
                            last.then_inc(sm["s_o"], 1)
                    if k < AU - 1:
                        scores(k + 1, 1)
                section_end(pe, "pe")

            for k in range(HK):
                for n in range(2):
                    pe.wait_ge(sm["s_xr"], 4 * n + 4)
                    for i in range(4):
                        last = pe.transpose(ps[:, 2 * k + n, i * P:(i + 1) * P],
                                            xr[:, 4 * n + i, k * P:(k + 1) * P], ident[:])
                    last.then_inc(sm["s_tr"], 1)
            pe.wait_ge(sm["s_trE"], 4)
            for t in range(NT):
                for k in range(HK):
                    last = mm(ps[:, 4, t * E:(t + 1) * E], xrT[:, k, t * P:(t + 1) * P], wgate[:, k, :],
                              start=(k == 0), stop=(k == HK - 1))
            last.then_inc(sm["s_ba"], 1)
            pe.wait_ge(sm["s_g"], 1)
            for t in range(NT):
                last = pe.transpose(ps[0:3 * (E + 1), 5 + t // 4, (t % 4) * P:(t % 4 + 1) * P],
                                    ws[:, t].rearrange("p a e -> p (a e)"), ident[:])
                if t % 4 == 3:
                    last.then_inc(sm["s_grT"], 1)
            section_end(pe, "pe")

            with pe.Fori(0, NG) as i:
                for j in range(FG):
                    for n in range(2):
                        u = 2 * j + n
                        cols = slice(n * 512, (n + 1) * 512)
                        if j:
                            pe.wait_ge(sm["s_act"], u - 1)
                        for part in range(2):
                            for k in range(HK):
                                last = mm(ps[:, 3 * n + part, :], w13[:, j, k, part * P:(part + 1) * P], xrT[:, k, cols],
                                          start=(k == 0), stop=(k == HK - 1))
                        mm(ps[:, 3 * n + 2, :], sel[:, j * P:(j + 1) * P], wT[:, cols],
                           start=True, stop=True).then_inc(sm["s_gu"], 1)
                for t in range(NT):
                    if t % 4 == 0:
                        pe.wait_ge(sm["s_act"], 2 * FG - 1 + t // 4)
                    if t >= 2:
                        pe.wait_ge(sm["s_dnE"], t - 1)
                    for j in range(FG):
                        last = mm(ps[:, 6 + t % 2, 0:H], act_t[:, j, t * P:(t + 1) * P], w2[:, j, :],
                                  start=(j == 0), stop=(j == FG - 1))
                    last.then_inc(sm["s_dn"], 1)
                section_end(pe, "pe")

            def flow_bank(flow, evacuated):
                if len(flow) >= 2:
                    s, v = flow[-2]
                    pe.wait_ge(sm[s], v)
                flow.append(evacuated)
                return 6 + (len(flow) - 1) % 2

            def transposes(bank, sources, s):
                for i, src in enumerate(sources):
                    last = pe.transpose(ps[:, bank, i * P:(i + 1) * P], src, ident[:])
                last.then_inc(sm[s], 1)

            def project(flow, u):
                i, b = (1, 0, 2, 3)[u // 2], u % 2
                bank = 4 + u if u < 2 else flow_bank(flow, ("s_conv", u + 1) if u < 4 else ("s_raw", u - 3))
                for k in range(HK):
                    last = mm(ps[:, bank, :], wA[:, k, i * P:(i + 1) * P], xnT[:, k, b * S:(b + 1) * S],
                              start=(k == 0), stop=(k == HK - 1))
                last.then_inc(sm["s_A"], 1)

            def key_products(nx):
                pe.wait_ge(sm["s_silu"], 4)
                for t in range(NT):
                    for c in range(2):
                        at = t * P + c * CH
                        for i, x in enumerate((kT[:, nx], qT)):
                            last = mm(ps[c * CH:(c + 1) * CH, 4 + t // 4, (t % 4) * P + i * CH:(t % 4) * P + (i + 1) * CH],
                                      kT[:, nx, at:at + CH], x[:, at:at + CH], start=True, stop=True)
                last.then_inc(sm["s_kq"], 1)

            def turn_keys(flow, nx, n):
                bank = flow_bank(flow, ("s_kd", n + 1))
                transposes(bank, [kT[:, nx, t * P:(t + 1) * P] for t in range(4 * n, 4 * n + 4)], "s_kt")

            def turn_queries(flow, n):
                bank = flow_bank(flow, ("s_sqq", n + 1))
                transposes(bank, [qT[:, t * P:(t + 1) * P] for t in range(4 * n, 4 * n + 4)], "s_qt")

            def turn_values(flow, u):
                pe.wait_ge(sm["s_silu"], 5 + u)
                bank = flow_bank(flow, ("s_vTE", u + 1))
                transposes(bank, [vT[:, u % 2, t * P:(t + 1) * P] for t in range(4)], "s_vt")

            def gate_product(flow, m):
                bank = flow_bank(flow, ("s_zE", m + 1))
                for b in range(B):
                    at = b * S + m * P
                    for k in range(HK):
                        last = mm(ps[:, bank, b * R * D:(b + 1) * R * D], xnT[:, k, at:at + P], wz[:, k, :],
                                  start=(k == 0), stop=(k == HK - 1))
                last.then_inc(sm["s_z"], 1)

            def turn_outputs(flow, m):
                pe.wait_ge(sm["s_gate"], 2 * m + 2)
                bank = flow_bank(flow, ("s_xE", m + 1))
                transposes(bank, [xo[:, m % 2, b * R + r, :] for r in range(R) for b in range(B)], "s_x")

            def output_product(par, t):
                if t >= 2:
                    pe.wait_ge(sm["s_woE"], t - 1)
                for r in range(R):
                    last = mm(ps[:, output_bank(t), r * H:(r + 1) * H], xT[:, 1 - par, r, t * P:(t + 1) * P],
                              wout[:, r, :], start=True, stop=True)
                last.then_inc(sm["s_wo"], 1)

            def level(lhs, rhs, at, s, ready):
                for r in range(R):
                    for sname, v in ready:
                        pe.wait_ge(sm[sname], v(r))
                    for t in range(NT):
                        last = mm(ps[:, 4 + r, at + t * BL:at + (t + 1) * BL], lhs[:, r, t, :], rhs[:, r, t, :],
                                  start=True, stop=True)
                    last.then_inc(sm[s], 1)

            def first_products():
                level(MTbd, Tc, 0, "s_xa", [("s_bd", lambda r: 4 * R), ("s_tt", lambda r: r + 1)])

            def blocks_of_32():
                level(TTbd, Xc, 256, "s_pa", [("s_xaE", lambda r: r + 1)])

            def beside_products():
                level(MOFF, Tc, 0, "s_xb", [("s_paE", lambda r: r + 1)])

            def chunks_from_32():
                level(TTbd, Xc, 256, "s_pb", [("s_xbE", lambda r: r + 1), ("s_tt2", lambda r: r + 1)])

            def solve_products(flow):
                for u in range(R * NT // 2):
                    r, m = u // 4, u % 4
                    pe.wait_ge(sm["s_pbE"], r + 1)
                    bank = flow_bank(flow, (("s_yE", "s_yF")[u % 2], u // 2 + 1))
                    for i in range(2):
                        last = mm(ps[:, bank, i * (CH + D):(i + 1) * (CH + D)], T64[:, r, 2 * m + i, :],
                                  BK[:, r, 2 * m + i, :], start=True, stop=True)
                    last.then_inc(sm["s_y"], 1)

            flow = []
            pe.wait_ge(sm["s_w"], 16 * 10)
            for u in range(4):
                project(flow, u)
            key_products(0)
            for n in range(2):
                turn_queries(flow, n)
            for n in range(2):
                turn_keys(flow, 0, n)
            for u in (4, 5):
                project(flow, u)
            for u in (0, 1):
                turn_values(flow, u)
            for u in (6, 7):
                project(flow, u)
            for u in (2, 3):
                turn_values(flow, u)
            pe.wait_ge(sm["s_at"], R)
            first_products()
            blocks_of_32()
            beside_products()
            chunks_from_32()
            solve_products(flow)
            section_end(pe, "pe")

            def gdn_body(i, par, last_body):
                nx = 1 - par
                flow = []

                def pre(f, *a):
                    if not last_body:
                        f(*a)

                def key_state(n, b):
                    pe.wait_ge(sm["s_S"], 2 * (n - 1) + b + 1)
                    rows = slice((n % 2) * CH, (n % 2 + 1) * CH)
                    at = b * S + n * CH
                    for r in range(R):
                        last = mm(ps[rows, b, r * D:(r + 1) * D], kT[:, par, at:at + CH], St[:, n % 2, b * R + r, :],
                                  start=True, stop=True)
                    last.then_inc(sm["s_p1"], 1)

                def residual(n, b, r):
                    rows = slice((n % 2) * CH, (n % 2 + 1) * CH)
                    return Rb[rows, b * R + r, :] if n else vs[rows, par, r, 4 * b, :]

                def new_state(n, b):
                    if n:
                        pe.wait_ge(sm["s_R"], 2 * (n - 1) + b + 1)
                    rows = slice((n % 2) * CH, (n % 2 + 1) * CH)
                    for r in range(R):
                        last = mm(ps[:, b, (R + r) * D:(R + r + 1) * D], AW[rows, par, r, 4 * b + n // 2, CH:],
                                  residual(n, b, r), start=True, stop=True)
                    last.then_inc(sm["s_p2"], 1)

                def chunk_output(n, b):
                    m, rows, at = n // 2, slice((n % 2) * CH, (n % 2 + 1) * CH), b * S + n * CH
                    if n == STEPS - 1:
                        pe.wait_ge(sm["s_R"], 2 * (n - 1) + b + 1)
                    if n % 2 == 0 and m:
                        pe.wait_ge(sm["s_gate"], 2 * (m - 1) + b + 1)
                    for r in range(R):
                        dst = ps[rows, 2 + b, r * D:(r + 1) * D]
                        if n:
                            mm(dst, qg[:, par, r, at:at + CH], St[:, n % 2, b * R + r, :], start=True, stop=False)
                        last = mm(dst, AW[rows, par, r, 4 * b + m, 0:CH], residual(n, b, r), start=(n == 0), stop=True)
                    last.then_inc(sm["s_O"], 1)

                def beside_residuals(n):
                    if n == 0:
                        for u in (0, 1):
                            pre(project, flow, u)
                    if n == 1:
                        gate_product(flow, 0)
                    if n == 2:
                        pre(key_products, nx)
                    if n == 3:
                        turn_outputs(flow, 0)
                    if n == 4:
                        gate_product(flow, 1)
                    if n == 6:
                        turn_outputs(flow, 1)
                        gate_product(flow, 2)
                    if n == 7:
                        turn_outputs(flow, 2)
                        gate_product(flow, 3)

                def beside_states(n):
                    if n == 0:
                        for u in (2, 3):
                            pre(project, flow, u)
                    if n == 2:
                        for k in range(2):
                            pre(turn_queries, flow, k)
                        for k in range(2):
                            pre(turn_keys, flow, nx, k)
                    if n == 3:
                        for u in (4, 5):
                            pre(project, flow, u)

                for n in range(STEPS):
                    if n:
                        for b in range(B):
                            key_state(n, b)
                    beside_residuals(n)
                    if n < STEPS - 1:
                        for b in range(B):
                            new_state(n, b)
                    beside_states(n)
                    for b in range(B):
                        chunk_output(n, b)
                    if n == 5:
                        for t in range(4):
                            output_product(par, t)
                pe.wait_ge(sm["s_woE"], 4)
                pre(first_products)
                pe.wait_ge(sm["s_R"], 2 * (STEPS - 1))
                for t in (4, 5):
                    output_product(par, t)
                pre(blocks_of_32)
                for u in (0, 1):
                    pre(turn_values, flow, u)
                for u in (6, 7):
                    pre(project, flow, u)
                turn_outputs(flow, 3)
                pre(beside_products)
                for t in (6, 7):
                    output_product(par, t)
                pre(chunks_from_32)
                for u in (2, 3):
                    pre(turn_values, flow, u)
                pre(solve_products, flow)
                section_end(pe, "pe")

            gdn_bodies(pe, gdn_body)
            for t in range(NT):
                output_product(0, t)
            section_end(pe, "pe")

        @block.scalar
        def _(act):
            fn = act.activation

            act.wait_ge(sm["s_eps"], 2)
            act.wait_ge(sm["s_stat"], 1)
            fn(sd[:], mv[:, :, 1], ACT.Sqrt, bias=eps5[:]).then_inc(sm["s_sd"], 1)
            for t in range(NT):
                act.wait_ge(sm["s_xn"], t + 1)
                if t:
                    act.wait_ge(sm["s_ssq"], t)
                fn(junk[:], xn[:, t, :], ACT.Square, accum_out=ssq[:, t:t + 1]).then_inc(sm["s_ssq"], 1)
            act.wait_ge(sm["s_ssq"], NT)
            fn(rms[:], ssq[:], ACT.Sqrt, bias=eps6[:], scale=1.0 / H).then_inc(sm["s_rms"], 1)
            for i in range(4):
                act.wait_ge(sm["s_tr"], i + 1)
                fn(xnT[:, i // 2, (i % 2) * 512:(i % 2 + 1) * 512], ps[:, i, :], ACT.Copy).then_inc(sm["s_trE"], 1)
            act.wait_ge(sm["s_g1"], 2)
            fn(gb[:], gb[:], ACT.Exp, scale=-1.0).then_inc(sm["s_g2"], 1)
            fn(gs[:], ba[:, :, 0:NV], ACT.Exp, scale=-1.0).then_inc(sm["s_g2"], 1)
            fn(alog[:], alog[:], ACT.Exp).then_inc(sm["s_g2"], 1)
            act.wait_ge(sm["s_g2"], 3)
            fn(gb[:], gb[:], ACT.Ln, bias=1.0).then_inc(sm["s_g3"], 1)
            act.wait_ge(sm["s_G"], 2)
            fn(ga[:], G[:], ACT.Exp).then_inc(sm["s_g2"], 1)
            fn(gc[:], gc[:], ACT.Exp).then_inc(sm["s_g2"], 1)
            act.wait_ge(sm["s_grT"], 2)
            fn(growT[:], ps[0:NV, 3:5, :].rearrange("p a n -> p (a n)"), ACT.Copy).then_inc(sm["s_grE"], 1)
            fn(erowT[:], ps[0:NV, 3:5, :].rearrange("p a n -> p (a n)"), ACT.Exp).then_inc(sm["s_grE"], 1)
            section_end(act, "act")

            def take_qk(k=0):
                for j in range(4):
                    act.wait_ge(sm["s_qk"], 4 * k + j + 1)
                    dst = (aqT, akT)[j // 2]
                    fn(dst[:, (j % 2) * 512:(j % 2 + 1) * 512], ps[:, 6 + j % 2, :], ACT.Copy).then_inc(sm["s_qkE"], 1)

            take_qk()
            section_end(act, "act")
            with act.Fori(0, NH // AU) as i:
                for k in range(AU):
                    for b in range(B):
                        act.wait_ge(sm["s_bias"], 2 * k + b + 1)
                        for qt in range(4):
                            u = 4 * b + qt
                            fn(prob[:, u, 0:(qt + 1) * P], score(b, qt), ACT.Exp, bias=bias[:, u:u + 1],
                               scale=ATT_SCALE, accum_out=psums[:, u:u + 1]).then_inc(sm["s_exp"], 1)
                    take_qk(k)
                    for b in range(B):
                        for kt in range(4):
                            act.wait_ge(sm["s_pT"], 8 * k + 4 * b + kt + 1)
                            fn(probT[:, 4 * b + kt, kt * P:S], ps[:, 3 * b + kt % 3, kt * P:S], ACT.Copy).then_inc(sm["s_pTE"], 1)
                    for b in range(B):
                        act.wait_ge(sm["s_pv"], 2 * k + b + 1)
                        fn(attT[:, b * S:(b + 1) * S], ps[:, 6 + b, :], ACT.Copy).then_inc(sm["s_pvE"], 1)
                section_end(act, "act")

            for t in range(NT):
                if t:
                    act.wait_ge(sm["s_ssq"], t)
                fn(junk[:], hid[:, t, :], ACT.Square, accum_out=ssq[:, t:t + 1]).then_inc(sm["s_ssq"], 1)
            act.wait_ge(sm["s_ssq"], NT)
            fn(rms[:], ssq[:], ACT.Sqrt, bias=eps6[:], scale=1.0 / H).then_inc(sm["s_rms"], 1)
            for i in range(4):
                act.wait_ge(sm["s_tr"], i + 1)
                k, n = i // 2, i % 2
                fn(xrT[:, k, n * 512:(n + 1) * 512], ps[:, i, :], ACT.Copy, scale=ln2[:, k:k + 1]).then_inc(sm["s_trE"], 1)
            act.wait_ge(sm["s_g1"], 1)
            fn(lg[:], lg[:], ACT.Exp).then_inc(sm["s_g2"], 1)
            section_end(act, "act")

            with act.Fori(0, NG) as i:
                for u in range(2 * FG):
                    act.wait_ge(sm["s_gu"], u + 1)
                    if u >= 2:
                        act.wait_ge(sm["s_su"], u - 1)
                    fn(sg[:, u % 2, :], ps[:, 3 * (u % 2), :], ACT.Silu).then_inc(sm["s_sg"], 1)
                section_end(act, "act")

            def tap(u, bank):
                i = (1, 0, 2, 3)[u // 2]
                act.wait_ge(sm["s_A"], u + 1)
                if u >= 4:
                    act.wait_ge(sm["s_silu"], u - 3)
                fn(cv[:, u % 4, :], ps[:, bank, :], ACT.Copy, scale=cw[:, i, TAPS - 1:TAPS]).then_inc(sm["s_tap"], 1)
                if u >= 4:
                    if u >= 6:
                        act.wait_ge(sm["s_vt"], u - 5)
                    fn(vT[:, u % 2, :], ps[:, bank, :], ACT.Copy).then_inc(sm["s_raw"], 1)

            def silu(u, nx):
                b = u % 2
                dst = (kT[:, nx, b * S:(b + 1) * S], qT[:, b * S:(b + 1) * S], vT[:, b, :], vT[:, b, :])[u // 2]
                if u < 4:
                    act.wait_ge(sm["s_conv"], u + 1)
                else:
                    act.wait_ge(sm["s_vconv"], u - 3)
                fn(dst, cv[:, u % 4, :], ACT.Silu).then_inc(sm["s_silu"], 1)

            def decays():
                act.wait_ge(sm["s_gsub"], 1)
                fn(dec[:], dec[:], ACT.Exp).then_inc(sm["s_E"], 1)

            def query_squares(n, bank):
                act.wait_ge(sm["s_qt"], n + 1)
                for t in range(4 * n, 4 * n + 4):
                    q = ps[:, bank, (t % 4) * P:(t % 4 + 1) * P]
                    last = fn(q, q, ACT.Square, accum_out=ss[:, 1, t:t + 1])
                last.then_inc(sm["s_sqq"], 1)

            def decayed_keys(n, nx, bank):
                act.wait_ge(sm["s_kt"], n + 1)
                if n == 0:
                    act.wait_ge(sm["s_cb"], 1)
                for t in range(4 * n, 4 * n + 4):
                    for r in range(R):
                        last = fn(BK[:, r, t, CH:], ps[:, bank, (t % 4) * P:(t % 4 + 1) * P], ACT.Copy,
                                  scale=cb[:, r, 1, t:t + 1])
                last.then_inc(sm["s_kd"], 1)

            def values(u, nx, bank):
                r, n = u // 2, u % 2
                act.wait_ge(sm["s_vt"], u + 1)
                for t in range(4 * n, 4 * n + 4):
                    last = fn(vs[:, nx, r, t, :], ps[:, bank, (t % 4) * P:(t % 4 + 1) * P], ACT.Copy, scale=nrm[:, 0, t:t + 1])
                last.then_inc(sm["s_vTE"], 1)

            def norms():
                act.wait_ge(sm["s_ssk"], 1)
                act.wait_ge(sm["s_sqq"], 2)
                fn(nrm[:], ss[:], ACT.Sqrt, bias=eps6[:]).then_inc(sm["s_nrm"], 1)

            def output_rms(par):
                fn(rms2[:], ss2[:, 1 - par], ACT.Sqrt, bias=eps6[:], scale=1.0 / D).then_inc(sm["s_nrm"], 1)

            def gate_silu(m, bank):
                act.wait_ge(sm["s_z"], m + 1)
                if m >= 2:
                    act.wait_ge(sm["s_gate"], 2 * (m - 1))
                fn(sz[:, m % 2].rearrange("p b d -> p (b d)"), ps[:, bank, :], ACT.Silu).then_inc(sm["s_zE"], 1)

            def output_squares(par, m):
                for b in range(B):
                    act.wait_ge(sm["s_gate"], 2 * m + b + 1)
                    for r in range(R):
                        if m:
                            act.wait_ge(sm["s_sqx"], 4 * (m - 1) + 2 * b + r + 1)
                        fn(junk_x[:, b * R + r, :], xo[:, m % 2, b * R + r, :], ACT.Square,
                           accum_out=ss2[:, par, r, 4 * b + m:4 * b + m + 1]).then_inc(sm["s_sqx"], 1)

            def outputs_turned(par, m, bank):
                act.wait_ge(sm["s_x"], m + 1)
                dst = xT[:, par].rearrange("p r (b n) -> p (r b) n", b=B)[:, :, m * P:(m + 1) * P]
                fn(dst, ps[:, bank, :].rearrange("p (a n) -> p a n", a=NC), ACT.Copy, scale=normw[:]).then_inc(sm["s_xE"], 1)

            def take_x(r, src, dst):
                act.wait_ge(sm[src], r + 1)
                fn(Xc[:, r], ps[:, 4 + r, 0:256].rearrange("p (t c) -> p t c", c=BL), ACT.Copy).then_inc(sm[dst], 1)

            def last_blocks(r):
                act.wait_ge(sm["s_pb"], r + 1)
                act.wait_ge(sm["s_t64"], r + 1)
                for q in (1, 3):
                    last = fn(T64[q * BL:(q + 1) * BL, r, :, (q - 1) * BL:q * BL],
                              ps[q * BL:(q + 1) * BL, 4 + r, 256:512].rearrange("p (t c) -> p t c", c=BL), ACT.Copy)
                last.then_inc(sm["s_pbE"], 1)

            def take_products(u, nx):
                r, m = u // 4, u % 4
                act.wait_ge(sm["s_y"], u + 1)
                fn(AW[:, nx, r, 2 * m:2 * m + 2, :],
                   ps[:, 6 + u % 2, 0:2 * (CH + D)].rearrange("p (t d) -> p t d", t=2), ACT.Copy).then_inc(sm["s_yE"], 1)

            def solved(nx):
                for r in range(R):
                    take_x(r, "s_xb", "s_xbE")
                for r in range(R):
                    last_blocks(r)
                for u in range(0, 8, 2):
                    take_products(u, nx)

            def bank_in(order, x):
                return {"p0": 4, "p1": 5}[x] if x in ("p0", "p1") else 6 + order.index(x) % 2

            order = flow_order(True, False)
            act.wait_ge(sm["s_w"], 16 * 10)
            decays()
            for u in range(4):
                tap(u, bank_in(order, "p%d" % u))
                silu(u, 0)
            for n in range(2):
                query_squares(n, bank_in(order, "q%d" % n))
            norms()
            for n in range(2):
                decayed_keys(n, 0, bank_in(order, "k%d" % n))
            act.wait_ge(sm["s_nrm"], 1)
            for u in (4, 5):
                tap(u, bank_in(order, "p%d" % u))
            silu(4, 0)
            silu(5, 0)
            for u in (0, 1):
                values(u, 0, bank_in(order, "v%d" % u))
            for u in (6, 7):
                tap(u, bank_in(order, "p%d" % u))
            silu(6, 0)
            silu(7, 0)
            for u in (2, 3):
                values(u, 0, bank_in(order, "v%d" % u))
            act.wait_ge(sm["s_gsub"], 2)
            fn(dec[:], dec[:], ACT.Exp)
            for r in range(R):
                take_x(r, "s_xa", "s_xaE")
            solved(0)
            section_end(act, "act")

            def gdn_body(i, par, last_body):
                nx = 1 - par
                order = flow_order(not last_body)

                def bank(x):
                    return bank_in(order, x)

                def taps(*units):
                    for u in units:
                        if not last_body:
                            tap(u, bank("p%d" % u))

                def silus(*units):
                    for u in units:
                        if not last_body:
                            silu(u, nx)

                def vals(*units):
                    for u in units:
                        if not last_body:
                            values(u, nx, bank("v%d" % u))

                taps(0, 1, 2, 3)
                silus(0, 1, 2)
                gate_silu(0, bank("z0"))
                silus(3)
                if not last_body:
                    query_squares(0, bank("q0"))
                    query_squares(1, bank("q1"))
                    norms()
                output_rms(par)
                for k in range(2):
                    if not last_body:
                        decayed_keys(k, nx, bank("k%d" % k))
                output_squares(par, 0)
                outputs_turned(par, 0, bank("x0"))
                taps(4, 5)
                gate_silu(1, bank("z1"))
                output_squares(par, 1)
                outputs_turned(par, 1, bank("x1"))
                gate_silu(2, bank("z2"))
                output_squares(par, 2)
                outputs_turned(par, 2, bank("x2"))
                gate_silu(3, bank("z3"))
                if not last_body:
                    for r in range(R):
                        take_x(r, "s_xa", "s_xaE")
                silus(4, 5)
                vals(0, 1)
                taps(6, 7)
                if not last_body:
                    decays()
                output_squares(par, 3)
                outputs_turned(par, 3, bank("x3"))
                if not last_body:
                    for r in range(R):
                        take_x(r, "s_xb", "s_xbE")
                silus(6, 7)
                if not last_body:
                    for r in range(R):
                        last_blocks(r)
                vals(2, 3)
                if not last_body:
                    for u in range(0, 8, 2):
                        take_products(u, nx)
                section_end(act, "act")

            gdn_bodies(act, gdn_body)
            output_rms(0)
            section_end(act, "act")

        @block.vector
        def _(dve):
            tt, ts, stt = dve.tensor_tensor, dve.tensor_scalar, dve.scalar_tensor_tensor
            steps = [0]

            def step(ins):
                steps[0] += 1
                ins.then_inc(sm["s_dch"], 1)
                dve.wait_ge(sm["s_dch"], steps[0])

            def end():
                steps[0] = 0
                section_end(dve, "dve")

            for t in range(NT):
                dve.wait_ge(sm["s_x"], 32)
                step(dve.bn_stats(stats[:, t, :], total[:, t, :]))
            for t in range(NT):
                last = dve.bn_aggr(mv[:, t, :], stats[:, t, :])
            last.then_inc(sm["s_stat"], 1)
            dve.wait_ge(sm["s_sd"], 1)
            step(dve.reciprocal(rstd[:], sd[:]))
            for t in range(NT):
                ts(xn[:, t, :], total[:, t, :], mv[:, t, 0:1], rstd[:, t:t + 1], ALU.subtract,
                   ALU.mult).then_inc(sm["s_xn"], 1)
            dve.wait_ge(sm["s_rms"], 1)
            step(dve.reciprocal(rrms[:], rms[:]))
            for t in range(NT):
                ts(xr[:, t, :], xn[:, t, :], rrms[:, t:t + 1], None, ALU.mult).then_inc(sm["s_xr"], 1)
            dve.wait_ge(sm["s_const"], 16 * 11)
            for i in range(4):
                dve.wait_ge(sm["s_tr"], 5 + i)
                k, n = i // 2, i % 2
                ts(xrT[:, k, n * 512:(n + 1) * 512], ps[:, 4 + i, :], ln1[:, k:k + 1], None,
                   ALU.mult).then_inc(sm["s_trE"], 1)
            dve.wait_ge(sm["s_ba"], 1)
            step(dve.tensor_copy(ba[:], ps[:, 0, :].rearrange("p (t v) -> p t v", t=NT)))
            step(tt(ga[:], ba[:, :, NV:2 * NV], dtb[:].unsqueeze(1).broadcast_to([P, NT, NV]), ALU.add))
            step(ts(gc[:], ga[:], -1.0, None, ALU.mult))
            tt(gb[:], ga[:], gc[:], ALU.max).then_inc(sm["s_g1"], 1)
            ts(ga[:], ga[:], 0.0, None, ALU.max).then_inc(sm["s_g1"], 1)
            dve.wait_ge(sm["s_g2"], 3)
            step(ts(gs[:], gs[:], 1.0, None, ALU.add))
            step(dve.reciprocal(gs[:], gs[:]))
            dve.wait_ge(sm["s_g3"], 1)
            step(tt(ga[:], ga[:], gb[:], ALU.add))
            stt(g[:], ga[:], -1.0, alog[:].unsqueeze(1).broadcast_to([P, NT, NV]), ALU.mult,
                ALU.mult).then_inc(sm["s_g"], 1)
            dve.wait_ge(sm["s_cum"], 2)
            cum, last_sum = (ps[:, i, 0:NT * NV].rearrange("p (t v) -> p t v", t=NT) for i in (1, 2))
            dve.tensor_copy(G[:], cum).then_inc(sm["s_G"], 1)
            dve.wait_ge(sm["s_G"], 1)
            tt(gc[:], last_sum, G[:], ALU.subtract).then_inc(sm["s_G"], 1)
            dve.wait_ge(sm["s_g2"], 5)

            def by_head(i):
                return gates[:, 0:NV, i, :].rearrange("p v t -> p t v")

            dve.memset(gates[:, NV:], 0.0)
            dve.tensor_copy(by_head(0), G[:])
            ts(by_head(1), ga[:], -1.0, None, ALU.mult)
            dve.tensor_copy(by_head(2), gs[:])
            tt(by_head(3), gs[:], gc[:], ALU.mult)
            end()
            end()

            def score_maxima(k, b):
                for i, qt in enumerate(SCORE_ORDER):
                    u = 4 * b + qt
                    dve.wait_ge(sm["s_sc"], 8 * k + 4 * b + max(i + 1, 2))
                    diag = score(b, qt)[:, qt * P:(qt + 1) * P]
                    tt(diag, diag, causal_neg[:], ALU.add).then_inc(sm["s_msk"], 1)
                    dve.wait_ge(sm["s_msk"], 8 * k + 4 * b + i + 1)
                    dve.tensor_reduce(nmax[:, u:u + 1], score(b, qt), AX.X, ALU.max).then_inc(sm["s_max"], 1)
                dve.wait_ge(sm["s_max"], 8 * k + 4 * b + 4)
                ts(bias[:, 4 * b:4 * b + 4], nmax[:, 4 * b:4 * b + 4], -ATT_SCALE, None, ALU.mult).then_inc(sm["s_bias"], 1)

            def add_outputs(k):
                for n in range(4):
                    dve.wait_ge(sm["s_o"], 4 * k + n + 1)
                    if k:
                        dve.wait_ge(sm["s_oE"], 4 * (k - 1) + n + 1)
                    rows = hid[:, 2 * n:2 * n + 2, :].rearrange("p t h -> p (t h)")
                    tt(rows, ps[:, 4 + n, :], rows, ALU.add).then_inc(sm["s_oE"], 1)

            with dve.Fori(0, NH // AU) as i:
                for k in range(AU):
                    score_maxima(k, 0)
                    if k:
                        add_outputs(k - 1)
                    score_maxima(k, 1)
                    for n in range(2):
                        dve.wait_ge(sm["s_v"], 2 * k + n + 1)
                        dve.tensor_copy(vt[:, 4 * n:4 * n + 4, :], ps[:, 6 + n, :].rearrange("p (t d) -> p t d", t=4))\
                           .then_inc(sm["s_vE"], 1)
                    for b in range(B):
                        dve.wait_ge(sm["s_exp"], 8 * k + 4 * b + 4)
                        dve.reciprocal(prec[:, 4 * b:4 * b + 4], psums[:, 4 * b:4 * b + 4]).then_inc(sm["s_rec"], 1)
                        dve.wait_ge(sm["s_rec"], 2 * k + b + 1)
                        for qt in range(4):
                            u = 4 * b + qt
                            p_row = prob[:, u, 0:(qt + 1) * P]
                            ts(p_row, p_row, prec[:, u:u + 1], None, ALU.mult).then_inc(sm["s_prob"], 1)
                add_outputs(AU - 1)
                end()

            dve.wait_ge(sm["s_rms"], 1)
            step(dve.reciprocal(rrms[:], rms[:]))
            for t in range(NT):
                ts(xr[:, t, :], hid[:, t, :], rrms[:, t:t + 1], None, ALU.mult).then_inc(sm["s_xr"], 1)
            tt(total[:], total[:], hid[:], ALU.add)
            dve.wait_ge(sm["s_ba"], 1)

            def over_experts(x):
                return x[:].unsqueeze(2).broadcast_to([P, NT, E])

            step(dve.tensor_copy(lg[:], ps[:, 4, 0:NT * E].rearrange("p (t e) -> p t e", t=NT)))
            step(dve.tensor_reduce(lmax[:], lg[:], AX.X, ALU.max))
            tt(lg[:], lg[:], over_experts(lmax), ALU.subtract).then_inc(sm["s_g1"], 1)
            dve.wait_ge(sm["s_g2"], 1)
            step(dve.tensor_reduce(lsum[:], lg[:], AX.X, ALU.add))
            step(dve.reciprocal(lrec[:], lsum[:]))
            step(tt(pr[:], lg[:], over_experts(lrec), ALU.mult))
            other = pr[:].unsqueeze(2).broadcast_to([P, NT, E, E])
            own = pr[:].unsqueeze(3).broadcast_to([P, NT, E, E])
            tt(cmp_a, other, own, ALU.is_gt)
            step(tt(cmp_b, other, own, ALU.is_equal))
            step(tt(cmp_b, cmp_b, before[:].unsqueeze(1).broadcast_to([P, NT, E, E]), ALU.mult))
            step(tt(cmp_a, cmp_a, cmp_b, ALU.add))
            step(dve.tensor_reduce(rank[:], cmp_a, AX.X, ALU.add))
            step(ts(keep[:], rank[:], TOPK - 0.5, None, ALU.is_lt))
            step(tt(keep[:], keep[:], pr[:], ALU.mult))
            step(dve.tensor_reduce(lsum[:], keep[:], AX.X, ALU.add))
            step(dve.reciprocal(lrec[:], lsum[:]))
            step(tt(wfull[:, :, 0:E], keep[:], over_experts(lrec), ALU.mult))
            step(dve.memset(wfull[:, :, E:E + 1], 1.0))
            left = [wfull[:], rest[:, 0], rest[:, 1]]
            for i in range(3):
                step(dve.tensor_copy(wh[:, :, i, :], left[i]))
                if i < 2:
                    step(dve.tensor_copy(ws[:, :, i, :], wh[:, :, i, :]))
                    step(tt(left[i + 1], left[i], ws[:, :, i, :], ALU.subtract))
                else:
                    dve.tensor_copy(ws[:, :, i, :], wh[:, :, i, :]).then_inc(sm["s_g"], 1)
            for n in range(2):
                dve.wait_ge(sm["s_grT"], n + 1)
                dve.tensor_copy(wT[:, n * 512:(n + 1) * 512], ps[0:3 * (E + 1), 5 + n, :])
            end()

            with dve.Fori(0, NG) as i:
                for u in range(2 * FG):
                    j, n = u // 2, u % 2
                    dve.wait_ge(sm["s_sg"], u + 1)
                    if u >= 2:
                        dve.wait_ge(sm["s_act"], u - 1)
                    tt(su[:, n, :], ps[:, 3 * n + 1, :], sg[:, n, :], ALU.mult).then_inc(sm["s_su"], 1)
                    dve.wait_ge(sm["s_su"], u + 1)
                    tt(act_t[:, j, n * 512:(n + 1) * 512], ps[:, 3 * n + 2, :], su[:, n, :],
                       ALU.mult).then_inc(sm["s_act"], 1)
                for t in range(NT):
                    dve.wait_ge(sm["s_dn"], t + 1)
                    tt(total[:, t, :], ps[:, 6 + t % 2, 0:H], total[:, t, :], ALU.add).then_inc(sm["s_dnE"], 1)
                end()

            def convolve(u, bank):
                i = (1, 0, 2, 3)[u // 2]
                for k in range(1, TAPS):
                    if k == 1:
                        dve.wait_ge(sm["s_tap"], u + 1)
                    else:
                        dve.wait_ge(sm["s_taps"], 2 * u + k - 1)
                    row = cv[:, u % 4, k:S]
                    stt(row, ps[:, bank, 0:S - k], cw[:, i, TAPS - 1 - k:TAPS - k], row, ALU.mult, ALU.add)\
                        .then_inc(sm["s_conv" if k == TAPS - 1 else "s_taps"], 1)

            def convolve_values(u):
                for k in range(1, TAPS):
                    if k == 1:
                        dve.wait_ge(sm["s_tap"], u + 1)
                        dve.wait_ge(sm["s_raw"], u - 3)
                    else:
                        dve.wait_ge(sm["s_vtaps"], 2 * (u - 4) + k - 1)
                    row = cv[:, u % 4, k:S]
                    stt(row, vT[:, u % 2, 0:S - k], cw[:, u // 2, TAPS - 1 - k:TAPS - k], row,
                        ALU.mult, ALU.add).then_inc(sm["s_vconv" if k == TAPS - 1 else "s_vtaps"], 1)

            def decay_exponents(nx, k=1):
                dve.wait_ge(sm["s_gm"], k)
                for r in range(R):
                    last = tt(dec[:, r], dec[:, r], gh[:, nx, r, 0, :].unsqueeze(2).broadcast_to([P, NT, CH]), ALU.subtract)
                last.then_inc(sm["s_gsub"], 1)
                dve.tensor_copy(eglast[:, nx], Ebc[:].rearrange("p r (a i) -> p r a i", i=CH)[:, :, :, CH - 1])\
                    .then_inc(sm["s_pre"], 1)

            kq = ps[:, 4:6, :].rearrange("p a (t m i) -> p (a t) m i", m=2, i=CH)

            def key_lengths(nx):
                dve.wait_ge(sm["s_kq"], 1)
                step(tt(diag_k[:], kq[:, :, 0, :], eye_c[:].unsqueeze(1).broadcast_to([P, NT, CH]), ALU.mult))
                dve.tensor_reduce(ss[:, 0, :], diag_k[:], AX.X, ALU.add).then_inc(sm["s_ssk"], 1)
                dve.wait_ge(sm["s_ssk"], 1)
                step(ts(rk2[:], ss[:, 0, :], 1e-6, None, ALU.add))
                step(dve.reciprocal(rk2[:], rk2[:]))
                tt(cb[:], gh[:, nx, :, 2:4, :], rk2[:].unsqueeze(1).unsqueeze(1).broadcast_to([P, R, 2, NT]), ALU.mult).then_inc(sm["s_cb"], 1)
                dve.wait_ge(sm["s_cb"], 1)

            def system(r):
                step(tt(dec[:, r], dec[:, r], cb[:, r, 0, :].unsqueeze(2).broadcast_to([P, NT, CH]), ALU.mult))
                for q in range(4):
                    rows, w = slice(q * BL, (q + 1) * BL), (q % 2) * BL
                    last = stt(MTc[rows, r], kq[rows, :, 0, w:w + BL], -1.0, dec[rows, r, :, w:w + BL], ALU.mult, ALU.mult)
                last.then_inc(sm["s_mt"], 1)

            def beside_and_attention(r):
                for q in (0, 2):
                    rows = slice(q * BL, (q + 1) * BL)
                    stt(MOFF[rows, r, :, (q + 1) * BL:(q + 2) * BL], kq[rows, :, 0, BL:2 * BL], -1.0,
                        dec[rows, r, :, BL:2 * BL], ALU.mult, ALU.mult)
                tt(BK[:, r, :, 0:CH], kq[:, :, 1, :], dec[:, r], ALU.mult).then_inc(sm["s_at"], 1)

            def query_scale(nx):
                dve.wait_ge(sm["s_nrm"], 1)
                step(dve.reciprocal(rq[:, nx], nrm[:, 1, :]))
                step(ts(rq[:, nx], rq[:, nx], D ** -0.5, None, ALU.mult))

            def solve_row(i):
                if i == 1:
                    step(dve.tensor_copy(Tb[:], eye16[:]))
                    dve.wait_ge(sm["s_blk"], 16 * 4)
                step(tt(Tprod[:, 0:i, 0:i], Tb[:, 0:i, 0:i].rearrange("p j c -> p c j"),
                        blk[:, 0:i, i].unsqueeze(1).broadcast_to([P, i, i]), ALU.mult))
                last = dve.tensor_reduce(Tb[:, i, 0:i], Tprod[:, 0:i, 0:i], AX.X, ALU.add)
                if i < SB - 1:
                    step(last)
                else:
                    last.then_inc(sm["s_solve"], 1)

            def transposed_blocks(r, s):
                for q in range(4):
                    rows = slice(q * BL, (q + 1) * BL)
                    last = dve.transpose(TTbd[rows, r, :, q * BL:(q + 1) * BL], Tc[rows, r])
                last.then_inc(sm[s], 1)

            def solved_blocks(r):
                dve.wait_ge(sm["s_tq"], 32)
                step(tt(Tc[:, r].rearrange("p t (w j) -> p t w j", w=2), Tq[:, r].unsqueeze(2).broadcast_to([P, NT, 2, SB]),
                        half[:].unsqueeze(1).unsqueeze(3).broadcast_to([P, NT, 2, SB]), ALU.mult))
                transposed_blocks(r, "s_tt")

            def blocks_of_32(r):
                dve.wait_ge(sm["s_pa"], r + 1)
                dve.copy_predicated(Tc[:, r].rearrange("p t c -> p (t c)"), m16[:], ps[:, 4 + r, 256:512])\
                    .then_inc(sm["s_paE"], 1)
                dve.wait_ge(sm["s_paE"], r + 1)
                transposed_blocks(r, "s_tt2")
                dve.wait_ge(sm["s_tt2"], r + 1)
                dve.transpose(T64[:, r].rearrange("p t c -> p (t c)"), TTbd[:, r].rearrange("p t c -> p (t c)"))\
                    .then_inc(sm["s_t64"], 1)

            def take_products(u, nx):
                r, m = u // 4, u % 4
                dve.wait_ge(sm["s_y"], u + 1)
                dve.tensor_copy(AW[:, nx, r, 2 * m:2 * m + 2, :],
                                ps[:, 6 + u % 2, 0:2 * (CH + D)].rearrange("p (t d) -> p t d", t=2)).then_inc(sm["s_yF"], 1)

            def output_scale(v):
                dve.wait_ge(sm["s_nrm"], v)
                step(dve.reciprocal(rr2[:], rms2[:]))

            def add_output(t):
                dve.wait_ge(sm["s_wo"], t + 1)
                for r in range(R):
                    if r:
                        dve.wait_ge(sm["s_wo1"], t + 1)
                    stt(total[:, t, :], ps[:, output_bank(t), r * H:(r + 1) * H], rr2[:, r, t:t + 1], total[:, t, :],
                        ALU.mult, ALU.add).then_inc(sm["s_woE" if r else "s_wo1"], 1)

            all_gates = gates[:].rearrange("p (k r) c t -> p k (r c t)", r=R)

            dve.wait_ge(sm["s_w"], 16 * 10)
            dve.wait_ge(sm["s_zero"], 3)
            step(dve.tensor_copy(gh[:, 0].rearrange("p r c t -> p (r c t)"), all_gates[:, 0, :]))
            decay_exponents(0)
            order = flow_order(True, False)

            def bank_in(order, x):
                return {"p0": 4, "p1": 5}[x] if x in ("p0", "p1") else 6 + order.index(x) % 2

            for u in range(4):
                convolve(u, bank_in(order, "p%d" % u))
            key_lengths(0)
            dve.wait_ge(sm["s_E"], 1)
            for r in range(R):
                system(r)
            for r in range(R):
                beside_and_attention(r)
            for u in range(4, 8):
                convolve_values(u)
            query_scale(0)
            for i in range(1, SB):
                solve_row(i)
            step(dve.tensor_copy(gh[:, 1].rearrange("p r c t -> p (r c t)"), all_gates[:, 1, :]))
            dve.wait_ge(sm["s_gl"], 16 * 6)
            decay_exponents(1, 2)
            for r in range(R):
                solved_blocks(r)
            for r in range(R):
                blocks_of_32(r)
            for u in range(1, 8, 2):
                take_products(u, 0)
            end()

            def gdn_body(i, par, last_body):
                nx = 1 - par
                order = flow_order(not last_body)

                def bank(x):
                    return bank_in(order, x)

                def residuals(n, b):
                    rows, t = slice((n % 2) * CH, (n % 2 + 1) * CH), 4 * b + n // 2
                    dve.wait_ge(sm["s_p1"], 2 * (n - 1) + b + 1)
                    for r in range(R):
                        last = stt(Rb[rows, b * R + r, :], ps[rows, b, r * D:(r + 1) * D], gh[rows, par, r, 1, t:t + 1],
                                   vs[rows, par, r, t, :], ALU.mult, ALU.add)
                    last.then_inc(sm["s_R"], 1)

                def states(n, b):
                    now = n % 2
                    dve.wait_ge(sm["s_p2"], 2 * n + b + 1)
                    new = ps[:, b, R * D:2 * R * D]
                    if n == 0:
                        last = dve.tensor_copy(St[:, 1, b * R:(b + 1) * R, :].rearrange("p r d -> p (r d)"), new)
                    else:
                        for r in range(R):
                            a = 2 * (4 * b + n // 2) + n % 2
                            last = stt(St[:, 1 - now, b * R + r, :], St[:, now, b * R + r, :], eglast[:, par, r, a:a + 1],
                                       new[:, r * D:(r + 1) * D], ALU.mult, ALU.add)
                    last.then_inc(sm["s_S"], 1)

                def gate(m):
                    dve.wait_ge(sm["s_zE"], m + 1)
                    if m >= 2:
                        dve.wait_ge(sm["s_x"], m - 1)
                        dve.wait_ge(sm["s_sqx"], 4 * (m - 1))
                    for b in range(B):
                        t = 4 * b + m
                        dve.wait_ge(sm["s_O"], 2 * (2 * m + 1) + b + 1)
                        for r in range(R):
                            last = stt(xo[:, m % 2, b * R + r, :], ps[:, 2 + b, r * D:(r + 1) * D], rq[:, par, t:t + 1],
                                       sz[:, m % 2, b, r * D:(r + 1) * D], ALU.mult, ALU.mult)
                        last.then_inc(sm["s_gate"], 1)

                def pre(f, *a):
                    if not last_body:
                        f(*a)

                def conv(*units):
                    for u in units:
                        if not last_body:
                            convolve(u, bank("p%d" % u))

                def solve_rows(a, b):
                    for k in range(a, b):
                        pre(solve_row, k)

                for n in range(STEPS):
                    if n:
                        for b in range(B):
                            residuals(n, b)
                    if n == 0:
                        conv(0)
                    if n == 1:
                        conv(3)
                    if n and n % 2 == 0:
                        gate(n // 2 - 1)
                    if n == 3:
                        for r in range(R):
                            pre(beside_and_attention, r)
                    if n < STEPS - 1:
                        for b in range(B):
                            states(n, b)
                    if n == 0:
                        conv(1, 2)
                    if n == 2:
                        pre(key_lengths, nx)
                        for r in range(R):
                            pre(system, r)
                    if n == 3:
                        solve_rows(1, 6)
                    if n == 4:
                        solve_rows(6, 10)
                        pre(query_scale, nx)
                        output_scale(1 if last_body else 2)
                    if n == 5:
                        solve_rows(10, SB)
                        for t in range(4):
                            add_output(t)
                if not last_body:
                    for r in range(R):
                        solved_blocks(r)
                if not last_body:
                    h = 2 * i + par + 2
                    src = all_gates[:, h, :] if isinstance(i, int) else all_gates[:, bass.ds(i * 2 + (par + 2), 1), :].squeeze(1)
                    dve.wait_ge(sm["s_gl"], 48)
                    dve.wait_ge(sm["s_R"], 2 * (STEPS - 1))
                    dve.wait_ge(sm["s_S"], 2 * (STEPS - 1))
                    step(dve.tensor_copy(gh[:, par].rearrange("p r c t -> p (r c t)"), src))
                    decay_exponents(par)
                gate(3)
                for u in (4, 5):
                    pre(convolve_values, u)
                for t in (4, 5):
                    add_output(t)
                if not last_body:
                    for r in range(R):
                        blocks_of_32(r)
                for u in (6, 7):
                    pre(convolve_values, u)
                for t in (6, 7):
                    add_output(t)
                if not last_body:
                    for u in range(1, 8, 2):
                        take_products(u, nx)
                end()

            gdn_bodies(dve, gdn_body)
            output_scale(1)
            for t in range(NT):
                add_output(t)
            end()

        @block.gpsimd
        def _(pool):
            pool.memset(eps5[:], 1e-5).then_inc(sm["s_eps"], 1)
            pool.memset(eps6[:], 1e-6).then_inc(sm["s_eps"], 1)
            pool.wait_ge(sm["s_xn"], NT)
            pool.tensor_copy(hid[:], xn[:])
            section_end(pool, "pool")
            section_end(pool, "pool")
            with pool.Fori(0, NH // AU) as i:
                section_end(pool, "pool")
            section_end(pool, "pool")
            with pool.Fori(0, NG) as i:
                section_end(pool, "pool")
            tt = pool.tensor_tensor

            def mask_decays():
                for r in range(R):
                    last = tt(dec[:, r], Gbc[:, r], e_neg[:].unsqueeze(1).broadcast_to([P, NT, CH]), ALU.add)
                last.then_inc(sm["s_gm"], 1)

            def prepare(nx):
                pool.wait_ge(sm["s_silu"], 4)
                for r in range(R):
                    tt(qg[:, nx, r], qT[:], Ebc[:, r], ALU.mult).then_inc(sm["s_qg"], 1)
                pool.wait_ge(sm["s_qg"], R)
                for i, q in enumerate((1, 3)):
                    pool.memset(MTbd[q * BL:(q + 1) * BL, :, :, (q - 1) * BL:q * BL], 0.0).then_inc(sm["s_rezero"], 1)
                    pool.wait_ge(sm["s_rezero"], i + 1)
                for r in range(R):
                    pool.wait_ge(sm["s_mt"], r + 1)
                    for q in range(4):
                        rows = slice(q * BL, (q + 1) * BL)
                        if r or q:
                            pool.wait_ge(sm["s_bd"], 4 * r + q)
                        pool.tensor_copy(MTbd[rows, r, :, q * BL:(q + 1) * BL], MTc[rows, r]).then_inc(sm["s_bd"], 1)
                pool.wait_ge(sm["s_bd"], 4 * R)

            pool.wait_ge(sm["s_w"], 16 * 10)
            pool.wait_ge(sm["s_gl"], 16 * 3)
            mask_decays()
            for x in (MTbd, MOFF, TTbd):
                pool.memset(x[:], 0.0).then_inc(sm["s_zero"], 1)
            for x in (xT[:, 1], ss2[:, 1]):
                pool.memset(x, 0.0)
            pool.wait_ge(sm["s_zero"], 3)
            prepare(0)
            pool.wait_ge(sm["s_gl"], 16 * 6)
            pool.wait_ge(sm["s_at"], R)
            mask_decays()
            section_end(pool, "pool")

            def gdn_body(i, par, last_body):
                if not last_body:
                    prepare(1 - par)
                    pool.wait_ge(sm["s_gl"], 48)
                    pool.wait_ge(sm["s_at"], R)
                    mask_decays()
                section_end(pool, "pool")

            gdn_bodies(pool, gdn_body)
            section_end(pool, "pool")


_OUT = (2, 512, 256)


def layout(x):
    import numpy as np
    c = np.ascontiguousarray

    def halves(a):
        return a.reshape(HK, P, -1).transpose(1, 0, 2)

    def wrap(a, n=1):
        return np.concatenate([a, a[:n]])

    qw = x["L0_ffn_q_w"].reshape(NH, 192, H)[:, :P]
    kvw = x["L0_ffn_kv_w"]
    kw, vw = kvw[:NH * P].reshape(NH, P, H), kvw[NH * P:2 * NH * P].reshape(NH, P, H)
    o = {"x": x["L0_attn_hidden_states"].reshape(TOK, H)}
    o["wqk"] = wrap(np.concatenate([qw, kw], 1).reshape(NH, 2 * P, HK, P).transpose(0, 3, 2, 1), 2)
    o["wv"] = wrap(vw.reshape(NH, P, HK, P).transpose(0, 3, 2, 1))
    o["wo"] = wrap(x["L0_ffn_o_w"].T.reshape(NH, P, H))
    o["ln1"] = x["L0_ffn_ln1_w"].reshape(HK, P).T
    o["ln2"] = x["L0_ffn_ln2_w"].reshape(HK, P).T
    o["wgate"] = halves(x["L0_ffn_gate_w"].T)
    pad = np.zeros((FT * P - E * I - SHI, H), np.float32)
    w1, sh = x["L0_ffn_w1"], x["L0_ffn_sh_gu_w"]
    gate_rows = np.concatenate([w1[:, :I].reshape(E * I, H), sh[:SHI], pad])
    up_rows = np.concatenate([w1[:, I:].reshape(E * I, H), sh[SHI:], pad])
    gu = np.concatenate([gate_rows.reshape(FT, P, H), up_rows.reshape(FT, P, H)], 1)
    gu = gu.reshape(NG, FG, 2 * P, HK, P).transpose(0, 4, 1, 3, 2)
    o["w13"] = wrap(gu)
    dn = np.concatenate([x["L0_ffn_w2"].transpose(0, 2, 1).reshape(E * I, H), x["L0_ffn_sh_down_w"].T, pad])
    o["w2"] = wrap(dn.reshape(NG, FG, P, H).transpose(0, 2, 1, 3))
    wba = x["L0_attn_W_ba"].reshape(H, NK, 2, R)
    o["wba"] = halves(wba.transpose(0, 2, 1, 3).reshape(H, 2 * NV))
    o["alog"], o["dtb"] = x["L0_attn_A_log"], x["L0_attn_dt_bias"]
    w = x["L0_attn_W_qkvz"].reshape(HK, P, NK, 4 * D + R * D).transpose(2, 1, 0, 3)
    o["wA"] = wrap(w[..., :4 * D], 2)
    o["wz"] = wrap(w[..., 4 * D:])
    cwt = x["L0_attn_conv_weight"]
    qc, kc, vc = (cwt[a:b].reshape(NK, -1, P, TAPS) for a, b in
                  ((0, NK * D), (NK * D, 2 * NK * D), (2 * NK * D, 2 * NK * D + NV * D)))
    o["cw"] = wrap(np.concatenate([qc, kc, vc], 1).transpose(0, 2, 1, 3), 2)
    wout = x["L0_attn_W_out"].reshape(NK, R, D, H).transpose(0, 2, 1, 3)
    o["wout"] = np.concatenate([wout[-1:], wout])
    o["normw"] = x["L0_attn_norm_weight"].reshape(D, 1)
    return {n: c(a) for n, a in o.items()} | constants()


def constants():
    import numpy as np
    from concourse import mybir as mb
    i = np.arange(P)
    same = i[:, None] // CH == i[None] // CH
    rows = np.minimum(np.arange(FT * P) // I, E)
    sel = (rows[None] == np.arange(E + 1)[:, None]).astype(np.float32)
    sel = np.tile(sel, (3, 1)).reshape(3 * (E + 1), NG, FG * P).transpose(1, 0, 2)
    e = np.arange(E)
    row, col = i[:, None] % BL, np.arange(BL)[None]
    m16 = np.tile(((row >= SB) & (col < SB)).astype(np.int32), (1, NT))
    src, dst = i[:, None] % CH, np.arange(CH)[None]
    return {
        "e_neg": np.where(src <= dst, 0.0, NEG).astype(np.float32),
        "eye_c": (src == dst).astype(np.float32),
        "eye16": np.tile(np.eye(SB, dtype=np.float32), (P, 1, 1)),
        "m16": m16,
        "half": (row // SB == np.arange(2)[None]).astype(np.float32),
        "ident": np.eye(P, dtype=np.float32),
        "cum_mask": (same & (i[:, None] <= i[None])).astype(np.float32),
        "chunk_ones": same.astype(np.float32),
        "causal_neg": np.where(i[None] <= i[:, None], 0.0, NEG).astype(np.float32),
        "before": np.tile((e[None] < e[:, None]).astype(np.float32), (P, 1, 1)),
        "sel": np.ascontiguousarray(np.concatenate([sel, sel[:1]])).astype(mb.dt.np(BF16)),
    }


def kernel(**inputs):
    import numpy as np
    import concourse.bacc as bacc
    from concourse.bass_utils import run_bass_kernel_spmd

    nc = bacc.Bacc("TRN2", target_bir_lowering=False, num_devices=1)
    arrays, d = {}, {}
    for name, a in layout({k: np.asarray(v) for k, v in inputs.items()}).items():
        arrays["in_" + name] = a
        d[name] = nc.dram_tensor("in_" + name, a.shape, mybir.dt.from_np(a.dtype), kind="ExternalInput").ap()
    out = nc.dram_tensor("out_0", [TOK, H], F32, kind="ExternalOutput").ap()
    build(nc, d, out)
    r = run_bass_kernel_spmd(nc, [arrays], core_ids=[0])
    return r.results[0]["out_0"].reshape(_OUT)
```
